# Optimizing a Trainium2 kernel written in Bass

```python
import numpy as np
import jax
import jax.numpy as jnp

def _softmax(x, axis=-1):
    return jax.nn.softmax(x, axis=axis)

def _gelu(x):
    return jax.nn.gelu(x, approximate=True)

def _silu(x):
    return jax.nn.silu(x)

def _sigmoid(x):
    return jax.nn.sigmoid(x)

def _layernorm(x, axis=-1, eps=1e-05):
    m = jnp.mean(x, axis=axis, keepdims=True)
    v = jnp.var(x, axis=axis, keepdims=True)
    return (x - m) / jnp.sqrt(v + eps)

def _scatter_add(tgt, idx, src, axis=0):
    return tgt.at[idx].add(src)

def _segment_sum(src, seg, n):
    return jax.ops.segment_sum(src, seg, n)
kernel_name = 'mk_xattn_ffn_d1_seqx_r2_02179f'

def setup_inputs(seed: int=0):
    np.random.seed(seed)
    _w = jnp.asarray

    def _rec_inputs():
        import jax
        import jax.numpy as jnp
        _rk = jax.random.key(seed)
        x = -0.0003929 + 0.9999 * jax.random.normal(jax.random.fold_in(_rk, 1), (32, 512, 512), jnp.float32)
        _lenS = 512 - jax.random.randint(jax.random.fold_in(_rk, 7), (32,), 0, max(1, 512 // 4) + 1, jnp.int32)
        _lenS2 = 512 - jax.random.randint(jax.random.fold_in(_rk, 8), (32,), 0, max(1, 512 // 4) + 1, jnp.int32)
        _ctx_1024P = jax.random.normal(jax.random.fold_in(_rk, 11), (32, 16, 512), jnp.float32)
        _ctx_1024c = jax.random.dirichlet(jax.random.fold_in(_rk, 511), 0.3 * jnp.ones((16,), jnp.float32), (32, 512))
        _ctx_1024t = jnp.einsum('bsk,bkd->bsd', _ctx_1024c, _ctx_1024P)
        _ctx_1024t = _ctx_1024t * jax.lax.rsqrt(jnp.mean(jnp.square(_ctx_1024t)) + 1e-12) * 0.953939
        ctx_1024 = 2.81802e-05 + 1.00001 * (_ctx_1024t + 0.3 * jax.random.normal(jax.random.fold_in(_rk, 611), (32, 512, 512), jnp.float32))
        return (x, ctx_1024)
    x, ctx_1024 = _rec_inputs()

    def _L0_xattn_setup():
        import jax, jax.numpy as jnp
        import numpy as np
        D = 512
        key = jax.random.key(seed)
        ks = jax.random.split(key, 9)
        B, Nq, Nk = (8, 1024, 1024)
        s = 1.0 / np.sqrt(D)
        return {'query': jax.random.normal(ks[0], (B, Nq, D), jnp.float32), 'key': jax.random.normal(ks[1], (B, Nk, D), jnp.float32), 'value': jax.random.normal(ks[2], (B, Nk, D), jnp.float32), 'Wq': jax.random.uniform(ks[3], (D, D), jnp.float32, -s, s), 'bq': jax.random.uniform(ks[4], (D,), jnp.float32, -s, s), 'Wk': jax.random.uniform(ks[5], (D, D), jnp.float32, -s, s), 'bk': jax.random.uniform(ks[6], (D,), jnp.float32, -s, s), 'Wv': jax.random.uniform(ks[7], (D, D), jnp.float32, -s, s), 'bv': jax.random.uniform(ks[8], (D,), jnp.float32, -s, s)}
    _L0_xattn_all = _L0_xattn_setup()
    _L0_xattn_in = {k: v for k, v in _L0_xattn_all.items() if k in ('Wq', 'bq', 'Wk', 'bk', 'Wv', 'bv')}
    del _L0_xattn_all

    def _L0_ffn_setup():
        import jax, jax.numpy as jnp
        import numpy as np
        ALPHA = 1.0
        key = jax.random.key(seed)
        ks = jax.random.split(key, 7)
        B, S, IN, OUT = (8, 4096, 512, 512)
        RANK, DDIM, UDIM = (4, 100, 50)
        return {'hidden_states': jax.random.normal(ks[0], (B, S, IN), dtype=jnp.float32), 'W': jax.random.normal(ks[1], (OUT, IN), dtype=jnp.float32) * 0.02, 'b': jax.random.normal(ks[2], (OUT,), dtype=jnp.float32) * 0.02, 'lora_down': jax.random.normal(ks[3], (RANK, DDIM), dtype=jnp.float32) * 0.1, 'lora_up': jax.random.normal(ks[4], (UDIM, RANK), dtype=jnp.float32) * 0.1, 'down_aux': jax.random.normal(ks[5], (DDIM, IN), dtype=jnp.float32) * 0.03, 'up_aux': jax.random.normal(ks[6], (OUT, UDIM), dtype=jnp.float32) * 0.03}
    _L0_ffn_all = _L0_ffn_setup()
    _L0_ffn_in = {k: v for k, v in _L0_ffn_all.items() if k in ('W', 'b', 'lora_down', 'lora_up', 'down_aux', 'up_aux')}
    del _L0_ffn_all
    return {'x': x, 'ctx_1024': ctx_1024, 'L0_xattn_Wq': _L0_xattn_in['Wq'], 'L0_xattn_bq': _L0_xattn_in['bq'], 'L0_xattn_Wk': _L0_xattn_in['Wk'], 'L0_xattn_bk': _L0_xattn_in['bk'], 'L0_xattn_Wv': _L0_xattn_in['Wv'], 'L0_xattn_bv': _L0_xattn_in['bv'], 'L0_ffn_W': _L0_ffn_in['W'], 'L0_ffn_b': _L0_ffn_in['b'], 'L0_ffn_lora_down': _L0_ffn_in['lora_down'], 'L0_ffn_lora_up': _L0_ffn_in['lora_up'], 'L0_ffn_down_aux': _L0_ffn_in['down_aux'], 'L0_ffn_up_aux': _L0_ffn_in['up_aux']}

def reference(x, ctx_1024, L0_xattn_Wq, L0_xattn_bq, L0_xattn_Wk, L0_xattn_bk, L0_xattn_Wv, L0_xattn_bv, L0_ffn_W, L0_ffn_b, L0_ffn_lora_down, L0_ffn_lora_up, L0_ffn_down_aux, L0_ffn_up_aux):
    import jax
    import jax.numpy as jnp

    def _L0_xattn_ref(query, key, value, Wq, bq, Wk, bk, Wv, bv):
        import jax, jax.numpy as jnp
        import numpy as np
        D = 512
        q = jnp.einsum('bnd,ed->bne', query, Wq) + bq
        k = jnp.einsum('bnd,ed->bne', key, Wk) + bk
        v = jnp.einsum('bnd,ed->bne', value, Wv) + bv
        scores = jnp.einsum('bqd,bkd->bqk', q, k)
        attn = jax.nn.softmax(scores, axis=-1)
        return jnp.einsum('bqk,bkd->bqd', attn, v)

    def _L0_ffn_ref(hidden_states, W, b, lora_down, lora_up, down_aux, up_aux):
        import jax, jax.numpy as jnp
        import numpy as np
        ALPHA = 1.0
        lilora_weight = up_aux @ (lora_up @ (lora_down @ down_aux))
        base = jnp.einsum('bsi,oi->bso', hidden_states, W) + b
        delta = jnp.einsum('bsi,oi->bso', hidden_states, lilora_weight)
        return base + ALPHA * delta
    x = x + _L0_xattn_ref(_layernorm(x, axis=-1), ctx_1024, ctx_1024, L0_xattn_Wq, L0_xattn_bq, L0_xattn_Wk, L0_xattn_bk, L0_xattn_Wv, L0_xattn_bv)
    x = x + _L0_ffn_ref(_layernorm(x, axis=-1), L0_ffn_W, L0_ffn_b, L0_ffn_lora_down, L0_ffn_lora_up, L0_ffn_down_aux, L0_ffn_up_aux)
    return x

_drawn_inputs = setup_inputs


def setup_inputs(seed=0):
    import zlib

    import numpy as np

    out = dict(_drawn_inputs(seed))
    spreads = {}
    factors = {'L0_xattn_bk': 8.0,
     'L0_xattn_bv': 2.705,
     'L0_ffn_b': 3.658,
     'L0_ffn_lora_up': 2.779,
     'L0_ffn_up_aux': 2.762}
    for name, (base, spread) in spreads.items():
        noise = np.random.default_rng([zlib.crc32(name.encode()), seed]).standard_normal(out[name].shape)
        drawn = base * np.exp(spread * noise) if base else spread * noise
        out[name] = jnp.asarray(drawn.astype(out[name].dtype))
    for name, factor in factors.items():
        out[name] = (out[name] * factor).astype(out[name].dtype)
    return out
```

```python
from contextlib import ExitStack

import concourse.bass as bass
from concourse import mybir
from concourse.alu_op_type import AluOpType as ALU

F32 = mybir.dt.float32
F32R = mybir.dt.float32r
ACT = mybir.ActivationFunctionType
AX_X = mybir.AxisListType.X

P = 128
EPS = 1e-5


def xattn_ffn_kernel(nc, x, ctxT, wq, wk, wvT, wT, bq, bk, bv, b_ffn,
                     lora_downT, lora_upT, down_aux, up_auxT, out):
    B, S, D = x.shape
    NT = D // P
    assert S == D == NT * P and B % 2 == 0 and B >= 4
    DDIM, RANK = lora_downT.shape
    UDIM = up_auxT.shape[0]
    DMA = 16

    with ExitStack() as stack:
        def sb(name, shape, dt=F32):
            return stack.enter_context(nc.sbuf_tensor(name, shape, dt))

        def pair(name, shape):
            return sb(name + "_hi", shape, F32R), sb(name + "_lo", shape, F32R)

        def bank(name):
            return stack.enter_context(nc.psum_tensor(name, [P, 512], F32))

        def sem(name):
            return stack.enter_context(nc.semaphore(name))

        m_hi, m_lo = pair("m", [P, NT, D])
        wv_hi, wv_lo = pair("wv", [P, NT, D])
        wf_hi, wf_lo = pair("wf", [P, NT, D])
        ctx_hi, ctx_lo = pair("ctx", [P, NT, S])
        xnT_hi, xnT_lo = pair("xnT", [P, NT, S])
        gT_hi, gT_lo = pair("gT", [P, NT, S])
        v_hi, v_lo = pair("v", [P, NT, D])
        rowT_hi, rowT_lo = pair("rowT", [P, NT, NT, P])

        x_sb = sb("x_sb", [P, 2, NT, D])
        ctx_raw = sb("ctx_raw", [P, NT, S])
        xn = sb("xn", [P, NT, D])
        row = sb("row", [P, NT, D])
        y_sb = sb("y_sb", [P, 2, D])
        dots = sb("dots", [P, D])

        wk_raw = sb("wk_raw", [P, NT, D])
        wq_raw = x_sb[:, 1, :, :]
        wvT_raw = ctx_raw
        wfT_raw = row
        down_sb = sb("down_sb", [DDIM, D])
        up_sb = sb("up_sb", [UDIM, D])
        t1_sb = sb("t1_sb", [RANK, D])
        t2_sb = sb("t2_sb", [UDIM, D])
        ldT_sb = sb("ldT_sb", [DDIM, RANK])
        luT_sb = sb("luT_sb", [RANK, UDIM])
        bk_wide = sb("bk_wide", [P, NT, P])
        bq_col = sb("bq_col", [P, NT])
        bk_col = sb("bk_col", [P, NT])
        bv_rows = sb("bv_rows", [P, D])
        b_rows = sb("b_rows", [P, D])
        u_rows = sb("u_rows", [P, D])
        g_bias = sb("g_bias", [P, NT])
        bqbk = sb("bqbk", [P, 1])
        ident = sb("ident", [P, P])
        zeros = sb("zeros", [P, P])
        minus_half = sb("minus_half", [P, 1])

        stats = sb("stats", [P, NT, 6])
        mean_var = sb("mean_var", [P, NT, 2])
        var_eps = sb("var_eps", [P, NT])
        rstd = sb("rstd", [P, NT])
        stats1 = sb("stats1", [P, NT, 6])
        mean_var1 = sb("mean_var1", [P, NT, 2])
        var_eps1 = sb("var_eps1", [P, NT])
        rstd1 = sb("rstd1", [P, NT])
        q_dot_bk = sb("q_dot_bk", [P, 2, NT])
        top = sb("top", [P, NT])
        top_r = sb("top_r", [P, NT])
        shift = sb("shift", [P, NT])
        row_sum = sb("row_sum", [P, NT])
        inv_sum = sb("inv_sum", [P, NT])

        bank_gv = [bank("bank_gv0"), bank("bank_gv1")]
        bank_s = [bank("bank_s0"), bank("bank_s1")]
        bank_af = [bank("bank_af0"), bank("bank_af1")]
        bank_t = [bank("bank_t0"), bank("bank_t1")]

        wqk_in = sem("wqk_in")
        wv_in = sem("wv_in")
        zeros_set = sem("zeros_set")
        small_in = sem("small_in")
        wf_in = sem("wf_in")
        bias_in = sem("bias_in")
        ident_set = sem("ident_set")
        half_set = sem("half_set")
        bk_spread = sem("bk_spread")
        m_done = sem("m_done")
        m_hi_set = sem("m_hi_set")
        m_lo_set = sem("m_lo_set")
        vec_done = sem("vec_done")
        vec_set = sem("vec_set")
        t_done = sem("t_done")
        t_set = sem("t_set")
        wf_done = sem("wf_done")
        wf_sum = sem("wf_sum")
        wf_hi_set = sem("wf_hi_set")
        wf_lo_set = sem("wf_lo_set")
        wv_hi_set = sem("wv_hi_set")
        wv_lo_set = sem("wv_lo_set")

        ctx_in = sem("ctx_in")
        x_in = [sem(f"x_in{j}") for j in range(NT)]
        y_out = [sem(f"y_out{k}") for k in range(2)]

        g_done = sem("g_done")
        s_done = sem("s_done")
        v_done = sem("v_done")
        a_done = sem("a_done")
        f_done = sem("f_done")
        xnT_done = sem("xnT_done")
        pT_done = sem("pT_done")
        xn1T_done = sem("xn1T_done")

        g_hi_set, g_lo_set = sem("g_hi_set"), sem("g_lo_set")
        v_hi_set, v_lo_set = sem("v_hi_set"), sem("v_lo_set")
        xnT_hi_set, xnT_lo_set = sem("xnT_hi_set"), sem("xnT_lo_set")
        pT_hi_set, pT_lo_set = sem("pT_hi_set"), sem("pT_lo_set")
        xn1T_hi_set, xn1T_lo_set = sem("xn1T_hi_set"), sem("xn1T_lo_set")
        ctx_hi_set, ctx_lo_set = sem("ctx_hi_set"), sem("ctx_lo_set")

        stats_set = sem("stats_set")
        mean_set = sem("mean_set")
        stats_seen = sem("stats_seen")
        eps_set = sem("eps_set")
        rstd_set = sem("rstd_set")
        xn_set = sem("xn_set")
        q_dot_set = sem("q_dot_set")
        xbv_set = sem("xbv_set")
        top_set = sem("top_set")
        top_r_set = sem("top_r_set")
        shift_set = sem("shift_set")
        p_set = sem("p_set")
        inv_set = sem("inv_set")
        x1_set = sem("x1_set")
        stats1_set = sem("stats1_set")
        mean1_set = sem("mean1_set")
        eps1_set = sem("eps1_set")
        rstd1_set = sem("rstd1_set")
        xn1_set = sem("xn1_set")
        x1b_set = sem("x1b_set")
        y_set = sem("y_set")

        def count(b, j):
            return b * NT + (j + 1)

        def tile(j):
            return slice(j * P, (j + 1) * P)

        def full(t):
            return t.bitcast(F32)

        def spread(bank_):
            return bank_[:, :].rearrange("p (c q) -> p c q", c=NT)

        def every_batch(engine, step):
            step(0, 0, first=True)
            with engine.Fori(0, B // 2 - 1) as t:
                step(t, 1)
                step(t + 1, 0)
            step(B // 2 - 1, 1, last=True)

        block = stack.enter_context(nc.Block())

        @block.sync
        def _(sp):
            sp.dma_start(wq_raw, wq.rearrange("(c p) d -> p c d", p=P)).then_inc(wqk_in, DMA)
            sp.dma_start(wk_raw[:, :, :], wk.rearrange("(c p) d -> p c d", p=P)).then_inc(wqk_in, DMA)
            sp.dma_start(bq_col[:, :], bq).then_inc(small_in, DMA)
            sp.dma_start(bk_col[:, :], bk).then_inc(small_in, DMA)
            sp.dma_start(ldT_sb[:, :], lora_downT).then_inc(small_in, DMA)
            sp.dma_start(luT_sb[:, :], lora_upT).then_inc(small_in, DMA)
            sp.dma_start(down_sb[:, :], down_aux).then_inc(small_in, DMA)
            sp.dma_start(up_sb[:, :], up_auxT).then_inc(small_in, DMA)
            for j in range(NT):
                sp.dma_start(x_sb[:, 0, j, :], x[0, tile(j), :]).then_inc(x_in[j], DMA)
            sp.dma_start(bv_rows[:, :], bv).then_inc(bias_in, DMA)
            sp.dma_start(b_rows[:, :], b_ffn).then_inc(bias_in, DMA)
            sp.wait_ge(wv_lo_set, NT)
            sp.dma_start(ctx_raw[:, :, :], ctxT[0].rearrange("(c p) s -> p c s", p=P)).then_inc(ctx_in, DMA)

            def step(half, odd, first=False, last=False):
                b = half * 2 + odd
                if not last:
                    sp.wait_ge(ctx_lo_set, count(b, NT - 1))
                    sp.dma_start(ctx_raw[:, :, :], ctxT[b + 1].rearrange("(c p) s -> p c s", p=P)
                                 ).then_inc(ctx_in, DMA)
                if first:
                    sp.wait_ge(m_done, NT)
                    sp.wait_ge(vec_done, 1)
                for j in range(NT):
                    if not first:
                        sp.wait_ge(y_set, count(b - 1, j))
                        sp.dma_start(out[b - 1, tile(j), :], y_sb[:, j % 2, :]).then_inc(y_out[j % 2], DMA)
                    if not last:
                        sp.dma_start(x_sb[:, 1 - odd, j, :], x[b + 1, tile(j), :]).then_inc(x_in[j], DMA)

            every_batch(sp, step)
            for j in range(NT):
                sp.wait_ge(y_set, count(B - 1, j))
                sp.dma_start(out[B - 1, tile(j), :], y_sb[:, j % 2, :]).then_inc(y_out[j % 2], DMA)
            for k in range(2):
                sp.wait_ge(y_out[k], DMA * (1 + B * NT // 2))

        @block.scalar
        def _(act):
            act.dma_start(wvT_raw[:, :, :], wvT.rearrange("(c p) e -> p c e", p=P)).then_inc(wv_in, DMA)
            act.dma_start(wfT_raw[:, :, :], wT.rearrange("(c p) e -> p c e", p=P)).then_inc(wf_in, DMA)

            def hi_of_x(b, j):
                act.wait_ge(xnT_done, count(b, j))
                act.activation(xnT_hi[:, :, tile(j)], spread(bank_t[1]), ACT.Identity).then_inc(xnT_hi_set, 1)

            def hi_of_ctx(b, j):
                if j == 0:
                    act.wait_ge(ctx_in, (b + 1) * DMA)
                act.activation(ctx_hi[:, j, :], ctx_raw[:, j, :], ACT.Identity).then_inc(ctx_hi_set, 1)

            act.wait_ge(wv_in, DMA)
            for c in range(NT):
                act.activation(wv_hi[:, c, :], wvT_raw[:, c, :], ACT.Identity).then_inc(wv_hi_set, 1)
            for c in range(NT):
                act.wait_ge(m_done, c + 1)
                act.activation(m_hi[:, c, :], bank_gv[c % 2][:, :], ACT.Identity).then_inc(m_hi_set, 1)
            for c in range(NT):
                act.wait_ge(wf_sum, c + 1)
                act.activation(wf_hi[:, c, :], wfT_raw[:, c, :], ACT.Identity).then_inc(wf_hi_set, 1)
            for j in range(NT):
                hi_of_x(0, j)
            for j in range(NT):
                hi_of_ctx(0, j)

            def step(half, odd, first=False, last=False):
                b = half * 2 + odd

                def hi_of_g(j):
                    act.wait_ge(g_done, count(b, j))
                    act.activation(gT_hi[:, j, :], bank_gv[j % 2][:, :], ACT.Identity,
                                   bias=g_bias[:, j:j + 1]).then_inc(g_hi_set, 1)

                def hi_of_x1(j):
                    act.wait_ge(xn1T_done, count(b - 1, j))
                    act.activation(rowT_hi[:, j, :, :], spread(bank_t[j % 2]), ACT.Identity
                                   ).then_inc(xn1T_hi_set, 1)

                hi_of_g(0)
                hi_of_g(1)
                if not first:
                    hi_of_x1(0)
                    hi_of_x1(1)
                hi_of_g(2)
                if not first:
                    hi_of_x1(2)
                    hi_of_x1(3)
                hi_of_g(3)
                for j in range(NT):
                    act.wait_ge(shift_set, count(b, j))
                    act.activation(row[:, j, :], bank_s[j % 2][:, :], ACT.Exp, bias=shift[:, j:j + 1],
                                   accum_out=row_sum[:, j:j + 1]).then_inc(p_set, 1)
                for j in range(NT):
                    act.wait_ge(v_done, count(b, j))
                    act.activation(v_hi[:, j, :], bank_gv[j % 2][:, :], ACT.Identity).then_inc(v_hi_set, 1)
                    act.wait_ge(pT_done, count(b, j))
                    act.activation(rowT_hi[:, j, :, :], spread(bank_t[0]), ACT.Identity).then_inc(pT_hi_set, 1)
                    if not last:
                        hi_of_x(b + 1, j)
                if not last:
                    for j in range(NT):
                        hi_of_ctx(b + 1, j)

            every_batch(act, step)
            for j in range(NT):
                act.wait_ge(xn1T_done, count(B - 1, j))
                act.activation(rowT_hi[:, j, :, :], spread(bank_t[j % 2]), ACT.Identity).then_inc(xn1T_hi_set, 1)

        @block.gpsimd
        def _(pool):
            pool.memset(ident[:, :], 0.0).then_inc(ident_set, 1)
            pool.wait_ge(ident_set, 1)
            pool.affine_select(out=ident[:, :], in_=ident[:, :], compare_op=ALU.not_equal, fill=1.0, base=0,
                               pattern=[[-1, P]], channel_multiplier=1).then_inc(ident_set, 1)
            pool.memset(minus_half[:, :], -0.5).then_inc(half_set, 1)
            pool.wait_ge(half_set, 1)

            def rstd_of_x(b, j):
                pool.wait_ge(eps_set, count(b, j))
                pool.tensor_tensor(rstd[:, j:j + 1], var_eps[:, j:j + 1], minus_half[:, :], ALU.pow
                                   ).then_inc(rstd_set, 1)

            def add_bv(b, odd, j):
                pool.wait_ge(xn_set, count(b, j))
                pool.tensor_tensor(x_sb[:, odd, j, :], x_sb[:, odd, j, :], bv_rows[:, :], ALU.add
                                   ).then_inc(xbv_set, 1)

            def rows_of_x(b, odd):
                for j in range(NT):
                    rstd_of_x(b, j)
                    if j:
                        add_bv(b, odd, j - 1)
                add_bv(b, odd, NT - 1)

            pool.wait_ge(bias_in, 2 * DMA)
            rows_of_x(0, 0)

            def step(half, odd, first=False, last=False):
                b = half * 2 + odd

                def rstd_of_x1(j):
                    pool.wait_ge(eps1_set, count(b, j))
                    pool.tensor_tensor(rstd1[:, j:j + 1], var_eps1[:, j:j + 1], minus_half[:, :], ALU.pow
                                       ).then_inc(rstd1_set, 1)

                def add_b(j):
                    pool.wait_ge(xn1_set, count(b, j))
                    pool.tensor_tensor(x_sb[:, odd, j, :], x_sb[:, odd, j, :], b_rows[:, :], ALU.add
                                       ).then_inc(x1b_set, 1)

                if not last:
                    rows_of_x(b + 1, 1 - odd)
                for j in range(NT):
                    rstd_of_x1(j)
                    if j:
                        add_b(j - 1)
                add_b(NT - 1)

            every_batch(pool, step)

        @block.vector
        def _(dve):
            dve.memset(zeros[:, :], 0.0).then_inc(zeros_set, 1)
            dve.wait_ge(zeros_set, 1)
            for k in range(2):
                dve.sem_inc(y_out[k], DMA)
            dve.wait_ge(small_in, 6 * DMA)
            for c in range(NT):
                dve.tensor_scalar(bk_wide[:, c, :], zeros[:, :], bk_col[:, c:c + 1], None, ALU.add
                                  ).then_inc(bk_spread, 1)

            def lo_of(lo, whole, hi, done):
                dve.tensor_tensor(lo, whole, full(hi), ALU.subtract).then_inc(done, 1)

            def aggregation_waits(written, value):
                dve.wait_ge(written, value)
                dve.sem_inc(stats_seen, 1)

            def stats_of_x(b, odd, j):
                dve.wait_ge(x_in[j], (b + 1) * DMA)
                dve.bn_stats(stats[:, j, :], x_sb[:, odd, j, :]).then_inc(stats_set, 1)
                aggregation_waits(stats_set, count(b, j))
                dve.bn_aggr(mean_var[:, j, :], stats[:, j, :]).then_inc(mean_set, 1)
                dve.wait_ge(mean_set, count(b, j))
                dve.tensor_scalar(var_eps[:, j:j + 1], mean_var[:, j, 1:2], EPS, None, ALU.add
                                  ).then_inc(eps_set, 1)

            def norm_of_x(b, odd, j):
                dve.wait_ge(rstd_set, count(b, j))
                dve.tensor_scalar(xn[:, j, :], x_sb[:, odd, j, :], mean_var[:, j, 0:1], rstd[:, j:j + 1],
                                  ALU.subtract, ALU.mult).then_inc(xn_set, 1)

            def q_dot_bk_of_x(b, odd, j):
                dve.wait_ge(xn_set, count(b, j))
                if j:
                    dve.wait_ge(q_dot_set, count(b, j - 1))
                elif not (isinstance(b, int) and b == 0):
                    dve.wait_ge(q_dot_set, count(b - 1, NT - 1))
                dve.tensor_tensor_reduce(dots[:, :], xn[:, j, :], u_rows[:, :], 1.0, bqbk[:, :], ALU.mult,
                                         ALU.add, q_dot_bk[:, odd, j:j + 1]).then_inc(q_dot_set, 1)

            def lo_of_x(b, j):
                dve.wait_ge(xnT_hi_set, count(b, j))
                lo_of(xnT_lo[:, :, tile(j)], spread(bank_t[1]), xnT_hi[:, :, tile(j)], xnT_lo_set)

            def lo_of_ctx(b, j):
                dve.wait_ge(ctx_hi_set, count(b, j))
                lo_of(ctx_lo[:, j, :], ctx_raw[:, j, :], ctx_hi[:, j, :], ctx_lo_set)

            for c in range(NT):
                dve.wait_ge(wv_hi_set, c + 1)
                lo_of(wv_lo[:, c, :], wvT_raw[:, c, :], wv_hi[:, c, :], wv_lo_set)
            for j in range(NT):
                stats_of_x(0, 0, j)
                if j:
                    norm_of_x(0, 0, j - 1)
            norm_of_x(0, 0, NT - 1)
            dve.wait_ge(t_done, 1)
            dve.tensor_copy(t1_sb[:, :], bank_af[0][0:RANK, :]).then_inc(t_set, 1)
            dve.wait_ge(t_done, 2)
            dve.tensor_copy(t2_sb[:, :], bank_af[1][0:UDIM, :]).then_inc(t_set, 1)
            for c in range(NT):
                dve.wait_ge(m_hi_set, c + 1)
                lo_of(m_lo[:, c, :], bank_gv[c % 2][:, :], m_hi[:, c, :], m_lo_set)
            dve.wait_ge(vec_done, 1)
            dve.tensor_copy(u_rows[:, :], bank_s[0][:, :]).then_inc(vec_set, 1)
            dve.wait_ge(vec_done, 2)
            dve.tensor_copy(g_bias[:, :], bank_s[1][:, 0:NT]).then_inc(vec_set, 1)
            dve.tensor_copy(bqbk[:, :], bank_s[1][:, NT:NT + 1]).then_inc(vec_set, 1)
            for c in range(NT):
                dve.wait_ge(wf_done, c + 1)
                dve.wait_ge(wf_in, DMA)
                dve.tensor_tensor(wfT_raw[:, c, :], bank_af[c % 2][:, :], wfT_raw[:, c, :], ALU.add
                                  ).then_inc(wf_sum, 1)
            for c in range(NT):
                dve.wait_ge(wf_hi_set, c + 1)
                lo_of(wf_lo[:, c, :], wfT_raw[:, c, :], wf_hi[:, c, :], wf_lo_set)
            dve.wait_ge(vec_set, 3)
            for j in range(NT):
                lo_of_x(0, j)
                q_dot_bk_of_x(0, 0, j)
            for j in range(NT):
                lo_of_ctx(0, j)

            def step(half, odd, first=False, last=False):
                b = half * 2 + odd

                def lo_of_g(j):
                    dve.wait_ge(g_hi_set, count(b, j))
                    dve.scalar_tensor_tensor(gT_lo[:, j, :], bank_gv[j % 2][:, :], g_bias[:, j:j + 1],
                                             full(gT_hi[:, j, :]), ALU.add, ALU.subtract
                                             ).then_inc(g_lo_set, 1)

                def lo_of_x1(j):
                    dve.wait_ge(xn1T_hi_set, count(b - 1, j))
                    lo_of(rowT_lo[:, j, :, :], spread(bank_t[j % 2]), rowT_hi[:, j, :, :], xn1T_lo_set)

                lo_of_g(0)
                lo_of_g(1)
                if not first:
                    lo_of_x1(0)
                    lo_of_x1(1)
                lo_of_g(2)
                if not first:
                    lo_of_x1(2)
                    lo_of_x1(3)
                lo_of_g(3)
                if not first:
                    for j in range(NT):
                        y_of(half - 1 + odd, 1 - odd, b - 1, j)
                for j in range(NT):
                    dve.wait_ge(s_done, count(b, j))
                    dve.tensor_reduce(top[:, j:j + 1], bank_s[j % 2][:, :], AX_X, ALU.max).then_inc(top_set, 1)
                    dve.wait_ge(top_set, count(b, j))
                    dve.wait_ge(q_dot_set, count(b, j))
                    dve.tensor_tensor(top_r[:, j:j + 1], top[:, j:j + 1], q_dot_bk[:, odd, j:j + 1], ALU.add
                                      ).then_inc(top_r_set, 1)
                    dve.wait_ge(top_r_set, count(b, j))
                    dve.tensor_tensor(shift[:, j:j + 1], q_dot_bk[:, odd, j:j + 1], top_r[:, j:j + 1],
                                      ALU.subtract).then_inc(shift_set, 1)
                    if not last:
                        stats_of_x(b + 1, 1 - odd, j)
                        if j:
                            norm_of_x(b + 1, 1 - odd, j - 1)
                            q_dot_bk_of_x(b + 1, 1 - odd, j - 1)
                if not last:
                    norm_of_x(b + 1, 1 - odd, NT - 1)
                    q_dot_bk_of_x(b + 1, 1 - odd, NT - 1)
                for j in range(NT):
                    dve.wait_ge(v_hi_set, count(b, j))
                    lo_of(v_lo[:, j, :], bank_gv[j % 2][:, :], v_hi[:, j, :], v_lo_set)
                    dve.wait_ge(pT_hi_set, count(b, j))
                    lo_of(rowT_lo[:, j, :, :], spread(bank_t[0]), rowT_hi[:, j, :, :], pT_lo_set)
                    if not last:
                        lo_of_x(b + 1, j)
                dve.wait_ge(p_set, count(b, NT - 1))
                dve.reciprocal(inv_sum[:, :], row_sum[:, :]).then_inc(inv_set, 1)
                dve.wait_ge(inv_set, b + 1)
                for j in range(NT):
                    dve.wait_ge(a_done, count(b, j))
                    dve.wait_ge(xbv_set, count(b, j))
                    dve.scalar_tensor_tensor(x_sb[:, odd, j, :], bank_af[j % 2][:, :], inv_sum[:, j:j + 1],
                                             x_sb[:, odd, j, :], ALU.mult, ALU.add).then_inc(x1_set, 1)
                    dve.wait_ge(x1_set, count(b, j))
                    dve.bn_stats(stats1[:, j, :], x_sb[:, odd, j, :]).then_inc(stats1_set, 1)
                    aggregation_waits(stats1_set, count(b, j))
                    dve.bn_aggr(mean_var1[:, j, :], stats1[:, j, :]).then_inc(mean1_set, 1)
                    dve.wait_ge(mean1_set, count(b, j))
                    dve.tensor_scalar(var_eps1[:, j:j + 1], mean_var1[:, j, 1:2], EPS, None, ALU.add
                                      ).then_inc(eps1_set, 1)
                    if not last:
                        lo_of_ctx(b + 1, j)
                    dve.wait_ge(rstd1_set, count(b, j))
                    dve.tensor_scalar(row[:, j, :], x_sb[:, odd, j, :], mean_var1[:, j, 0:1],
                                      rstd1[:, j:j + 1], ALU.subtract, ALU.mult).then_inc(xn1_set, 1)

            def y_of(half, odd, b, j):
                dve.wait_ge(f_done, count(b, j))
                dve.wait_ge(x1b_set, count(b, j))
                dve.wait_ge(y_out[j % 2], (b * 2 + (1 + j // 2)) * DMA)
                dve.tensor_tensor(y_sb[:, j % 2, :], bank_af[j % 2][:, :], x_sb[:, odd, j, :], ALU.add
                                  ).then_inc(y_set, 1)

            every_batch(dve, step)
            for j in range(NT):
                dve.wait_ge(xn1T_hi_set, count(B - 1, j))
                lo_of(rowT_lo[:, j, :, :], spread(bank_t[j % 2]), rowT_hi[:, j, :, :], xn1T_lo_set)
            for j in range(NT):
                y_of(B // 2 - 1, 1, B - 1, j)

        @block.tensor
        def _(pe):
            def product(bank_, left, right, done):
                for c in range(NT):
                    (l_hi, l_lo), (r_hi, r_lo) = left(c), right(c)
                    pe.matmul(bank_[:, :], l_hi, r_hi, start=(c == 0), stop=False)
                    pe.matmul(bank_[:, :], l_hi, r_lo, start=False, stop=False)
                    last = pe.matmul(bank_[:, :], l_lo, r_hi, start=False, stop=(c == NT - 1))
                last.then_inc(done, 1)

            def transposes(bank_, source, done):
                for c in range(NT):
                    last = pe.transpose(bank_[:, tile(c)], source[:, tile(c)], ident[:, :])
                last.then_inc(done, 1)

            pe.wait_ge(small_in, 6 * DMA)
            pe.matmul(bank_af[0][0:RANK, :], ldT_sb[:, :], down_sb[:, :], start=True, stop=True).then_inc(t_done, 1)
            pe.wait_ge(t_set, 1)
            pe.matmul(bank_af[1][0:UDIM, :], luT_sb[:, :], t1_sb[:, :], start=True, stop=True).then_inc(t_done, 1)
            pe.wait_ge(wqk_in, 2 * DMA)
            for c in range(NT):
                if c >= 2:
                    pe.wait_ge(m_lo_set, c - 1)
                for e in range(NT):
                    last = pe.matmul(bank_gv[c % 2][:, :], wq_raw[:, e, tile(c)], wk_raw[:, e, :],
                                     start=(e == 0), stop=(e == NT - 1))
                last.then_inc(m_done, 1)
            pe.wait_ge(bk_spread, NT)
            for e in range(NT):
                last = pe.matmul(bank_s[0][:, :], bk_wide[:, e, :], wq_raw[:, e, :], start=(e == 0), stop=(e == NT - 1))
            last.then_inc(vec_done, 1)
            for c in range(NT + 1):
                for e in range(NT):
                    left = wk_raw[:, e, tile(c)] if c < NT else bk_wide[:, e, :]
                    last = pe.matmul(bank_s[1][:, c:c + 1], left, bq_col[:, e:e + 1], start=(e == 0), stop=(e == NT - 1))
            last.then_inc(vec_done, 1)
            pe.wait_ge(t_set, 2)
            for c in range(NT):
                if c >= 2:
                    pe.wait_ge(wf_sum, c - 1)
                pe.matmul(bank_af[c % 2][:, :], t2_sb[:, tile(c)], up_sb[:, :], start=True, stop=True
                          ).then_inc(wf_done, 1)
            pe.wait_ge(ident_set, 2)

            def transpose_x(b, j):
                pe.wait_ge(xn_set, count(b, j))
                if j:
                    pe.wait_ge(xnT_lo_set, count(b, j - 1))
                transposes(bank_t[1], xn[:, j, :], xnT_done)

            def transpose_x1(b, j):
                pe.wait_ge(xn1_set, count(b, j))
                transposes(bank_t[j % 2], row[:, j, :], xn1T_done)

            def ffn(b, j):
                pe.wait_ge(xn1T_lo_set, count(b, j))
                product(bank_af[j % 2], lambda c: (rowT_hi[:, j, c, :], rowT_lo[:, j, c, :]),
                        lambda c: (wf_hi[:, c, :], wf_lo[:, c, :]), f_done)

            for j in range(NT):
                transpose_x(0, j)
            pe.wait_ge(m_lo_set, NT)
            pe.wait_ge(vec_set, 3)
            pe.wait_ge(wv_lo_set, NT)
            pe.wait_ge(wf_lo_set, NT)

            def step(half, odd, first=False, last=False):
                b = half * 2 + odd

                def g(j):
                    if j >= 2:
                        pe.wait_ge(g_lo_set, count(b, j - 2))
                    elif not first:
                        pe.wait_ge(v_lo_set, count(b - 1, j + 2))
                    if j == 0:
                        pe.wait_ge(xnT_lo_set, count(b, NT - 1))
                    product(bank_gv[j % 2], lambda c: (m_hi[:, c, tile(j)], m_lo[:, c, tile(j)]),
                            lambda c: (xnT_hi[:, c, :], xnT_lo[:, c, :]), g_done)

                def x1T(j):
                    if first:
                        return
                    if j == 0:
                        pe.wait_ge(pT_lo_set, count(b - 1, NT - 1))
                    elif j == 1:
                        pe.wait_ge(xnT_lo_set, count(b, NT - 1))
                    else:
                        pe.wait_ge(xn1T_lo_set, count(b - 1, j - 2))
                    transpose_x1(b - 1, j)

                g(0)
                g(1)
                x1T(0)
                x1T(1)
                g(2)
                x1T(2)
                x1T(3)
                g(3)
                if not first:
                    for j in range(NT):
                        if j < 2:
                            pe.wait_ge(x1_set, count(b - 1, j + 2))
                        else:
                            pe.wait_ge(y_set, count(b - 1, j - 2))
                        ffn(b - 1, j)
                pe.wait_ge(g_lo_set, count(b, NT - 1))
                pe.wait_ge(ctx_lo_set, count(b, NT - 1))
                for j in range(NT):
                    if j >= 2 or not first:
                        pe.wait_ge(p_set, b * NT + (j - 1))
                    product(bank_s[j % 2], lambda c: (gT_hi[:, c, tile(j)], gT_lo[:, c, tile(j)]),
                            lambda c: (ctx_hi[:, c, :], ctx_lo[:, c, :]), s_done)
                for j in range(NT):
                    pe.wait_ge(*((v_lo_set, count(b, j - 2)) if j >= 2 else (g_lo_set, count(b, j + 2))))
                    product(bank_gv[j % 2], lambda c: (ctx_hi[:, c, tile(j)], ctx_lo[:, c, tile(j)]),
                            lambda c: (wv_hi[:, c, :], wv_lo[:, c, :]), v_done)
                    pe.wait_ge(p_set, count(b, j))
                    if j:
                        pe.wait_ge(pT_lo_set, count(b, j - 1))
                    elif not first:
                        pe.wait_ge(xn1T_lo_set, count(b - 1, 2))
                    transposes(bank_t[0], row[:, j, :], pT_done)
                    if not last:
                        if j == 0:
                            pe.wait_ge(*((xnT_lo_set, count(b, 3)) if first else (xn1T_lo_set, count(b - 1, 3))))
                        transpose_x(b + 1, j)
                pe.wait_ge(v_lo_set, count(b, NT - 1))
                for j in range(NT):
                    pe.wait_ge(pT_lo_set, count(b, j))
                    if j >= 2:
                        pe.wait_ge(x1_set, count(b, j - 2))
                    elif not first:
                        pe.wait_ge(y_set, count(b - 1, j + 2))
                    product(bank_af[j % 2], lambda c: (rowT_hi[:, j, c, :], rowT_lo[:, j, c, :]),
                            lambda c: (v_hi[:, c, :], v_lo[:, c, :]), a_done)

            every_batch(pe, step)
            for j in range(NT):
                if j == 0:
                    pe.wait_ge(pT_lo_set, count(B - 1, NT - 1))
                elif j >= 2:
                    pe.wait_ge(xn1T_lo_set, count(B - 1, j - 2))
                transpose_x1(B - 1, j)
            for j in range(NT):
                pe.wait_ge(*((x1_set, count(B - 1, j + 2)) if j < 2 else (y_set, count(B - 1, j - 2))))
                ffn(B - 1, j)


_OUT = (32, 512, 512)


def kernel(x, ctx_1024, L0_xattn_Wq, L0_xattn_bq, L0_xattn_Wk, L0_xattn_bk, L0_xattn_Wv, L0_xattn_bv,
           L0_ffn_W, L0_ffn_b, L0_ffn_lora_down, L0_ffn_lora_up, L0_ffn_down_aux, L0_ffn_up_aux):
    import numpy as np
    import concourse.bacc as bacc
    from concourse.bass_utils import run_bass_kernel_spmd

    def column(v):
        return np.asarray(v).reshape(-1, P).T

    def rows(v):
        return np.broadcast_to(np.asarray(v), (P, v.shape[0]))

    def transposed(w):
        return np.swapaxes(np.asarray(w), -1, -2)

    layouts = {
        "x": x,
        "ctxT": transposed(ctx_1024),
        "wq": L0_xattn_Wq,
        "wk": L0_xattn_Wk,
        "wvT": transposed(L0_xattn_Wv),
        "wT": transposed(L0_ffn_W),
        "bq": column(L0_xattn_bq),
        "bk": column(L0_xattn_bk),
        "bv": rows(L0_xattn_bv),
        "b_ffn": rows(L0_ffn_b),
        "lora_downT": transposed(L0_ffn_lora_down),
        "lora_upT": transposed(L0_ffn_lora_up),
        "down_aux": L0_ffn_down_aux,
        "up_auxT": transposed(L0_ffn_up_aux),
    }
    nc = bacc.Bacc("TRN2", target_bir_lowering=False, num_devices=1)
    arrays, args = {}, []
    for name, value in layouts.items():
        a = np.ascontiguousarray(value)
        arrays[f"in_{name}"] = a
        args.append(nc.dram_tensor(f"in_{name}", a.shape, mybir.dt.from_np(a.dtype), kind="ExternalInput").ap())
    args.append(nc.dram_tensor("out_0", _OUT, F32, kind="ExternalOutput").ap())
    xattn_ffn_kernel(nc, *args)
    r = run_bass_kernel_spmd(nc, [arrays], core_ids=[0])
    return r.results[0]["out_0"]
```

```python
from contextlib import ExitStack

import concourse.bass as bass
from concourse import mybir
from concourse.alu_op_type import AluOpType as ALU

F32 = mybir.dt.float32
F32R = mybir.dt.float32r
ACT = mybir.ActivationFunctionType
AX_X = mybir.AxisListType.X

P = 128
EPS = 1e-5


def xattn_ffn_kernel(nc, x, ctxT, wq, wk, wvT, wT, bq, bk, bv, b_ffn,
                     lora_downT, lora_upT, down_aux, up_auxT, out):
    B, S, D = x.shape
    NT = D // P
    assert S == D == NT * P and B % 2 == 0 and B >= 4
    DDIM, RANK = lora_downT.shape
    UDIM = up_auxT.shape[0]
    DMA = 16

    with ExitStack() as stack:
        def sb(name, shape, dt=F32):
            return stack.enter_context(nc.sbuf_tensor(name, shape, dt))

        def pair(name, shape):
            return sb(name + "_hi", shape, F32R), sb(name + "_lo", shape, F32R)

        def bank(name):
            return stack.enter_context(nc.psum_tensor(name, [P, 512], F32))

        def sem(name):
            return stack.enter_context(nc.semaphore(name))

        m_hi, m_lo = pair("m", [P, NT, D])
        wv_hi, wv_lo = pair("wv", [P, NT, D])
        wf_hi, wf_lo = pair("wf", [P, NT, D])
        ctx_hi, ctx_lo = pair("ctx", [P, NT, S])
        xnT_hi, xnT_lo = pair("xnT", [P, NT, S])
        gT_hi, gT_lo = pair("gT", [P, NT, S])
        v_hi, v_lo = pair("v", [P, NT, D])
        rowT_hi, rowT_lo = pair("rowT", [P, NT, NT, P])

        x_sb = sb("x_sb", [P, 2, NT, D])
        ctx_raw = sb("ctx_raw", [P, NT, S])
        xn = sb("xn", [P, NT, D])
        row = sb("row", [P, NT, D])
        y_sb = sb("y_sb", [P, 2, D])
        dots = sb("dots", [P, D])

        wk_raw = sb("wk_raw", [P, NT, D])
        wq_raw = x_sb[:, 1, :, :]
        wvT_raw = sb("wvT_raw", [P, NT, D])
        wfT_raw = row
        down_sb = sb("down_sb", [DDIM, D])
        up_sb = sb("up_sb", [UDIM, D])
        t1_sb = y_sb[0:RANK, 0, :]
        t2_sb = y_sb[0:UDIM, 1, :]
        ldT_sb = sb("ldT_sb", [DDIM, RANK])
        luT_sb = sb("luT_sb", [RANK, UDIM])
        bk_wide = sb("bk_wide", [P, NT, P])
        bq_col = sb("bq_col", [P, NT])
        bk_col = sb("bk_col", [P, NT])
        bv_rows = sb("bv_rows", [P, D])
        b_rows = sb("b_rows", [P, D])
        u_rows = sb("u_rows", [P, D])
        g_bias = sb("g_bias", [P, NT])
        bqbk = sb("bqbk", [P, 1])
        ident = sb("ident", [P, P])
        zeros = sb("zeros", [P, P])
        minus_half = sb("minus_half", [P, 1])

        stats = sb("stats", [P, NT, 6])
        mean_var = sb("mean_var", [P, NT, 2])
        var_eps = sb("var_eps", [P, NT])
        rstd = sb("rstd", [P, NT])
        minus_mean = sb("minus_mean", [P, NT])
        offset = sb("offset", [P, NT])
        stats1 = sb("stats1", [P, NT, 6])
        mean_var1 = sb("mean_var1", [P, NT, 2])
        var_eps1 = sb("var_eps1", [P, NT])
        rstd1 = sb("rstd1", [P, NT])
        minus_mean1 = sb("minus_mean1", [P, NT])
        offset1 = sb("offset1", [P, NT])
        q_dot_bk = sb("q_dot_bk", [P, 2, NT])
        top = sb("top", [P, NT])
        top_r = sb("top_r", [P, NT])
        shift = sb("shift", [P, NT])
        row_sum = sb("row_sum", [P, NT])
        inv_sum = sb("inv_sum", [P, NT])

        bank_gv = [bank("bank_gv0"), bank("bank_gv1")]
        bank_s = [bank("bank_s0"), bank("bank_s1")]
        bank_af = [bank("bank_af0"), bank("bank_af1")]
        bank_t = [bank("bank_t0"), bank("bank_t1")]

        bank_m = bank_gv + bank_af

        wqk_in = [sem(f"wqk_in{c}") for c in range(NT)]
        wv_in = sem("wv_in")
        zeros_set = sem("zeros_set")
        small_in = sem("small_in")
        lora_in = sem("lora_in")
        wf_in = sem("wf_in")
        bias_in = sem("bias_in")
        ident_set = sem("ident_set")
        half_set = sem("half_set")
        bk_spread = sem("bk_spread")
        m_done = sem("m_done")
        m_hi_set = sem("m_hi_set")
        m_lo_set = sem("m_lo_set")
        vec_done = sem("vec_done")
        vec_set = sem("vec_set")
        t_done = sem("t_done")
        t_set = sem("t_set")
        wf_done = sem("wf_done")
        wf_sum = sem("wf_sum")
        wf_hi_set = sem("wf_hi_set")
        wf_lo_set = sem("wf_lo_set")
        wv_hi_set = sem("wv_hi_set")
        wv_lo_set = sem("wv_lo_set")

        ctx_in = sem("ctx_in")
        x_in = [sem(f"x_in{j}") for j in range(NT)]
        y_out = [sem(f"y_out{k}") for k in range(2)]

        g_done = sem("g_done")
        s_done = sem("s_done")
        v_done = sem("v_done")
        a_done = sem("a_done")
        f_done = sem("f_done")
        xnT_done = sem("xnT_done")
        pT_done = sem("pT_done")
        xn1T_done = sem("xn1T_done")

        g_hi_set, g_lo_set = sem("g_hi_set"), sem("g_lo_set")
        v_hi_set, v_lo_set = sem("v_hi_set"), sem("v_lo_set")
        xnT_hi_set, xnT_lo_set = sem("xnT_hi_set"), sem("xnT_lo_set")
        pT_hi_set, pT_lo_set = sem("pT_hi_set"), sem("pT_lo_set")
        xn1T_hi_set, xn1T_lo_set = sem("xn1T_hi_set"), sem("xn1T_lo_set")
        ctx_hi_set, ctx_lo_set = sem("ctx_hi_set"), sem("ctx_lo_set")

        stats_set = sem("stats_set")
        mean_set = sem("mean_set")
        stats_seen = sem("stats_seen")
        eps_set = sem("eps_set")
        minus_mean_set = sem("minus_mean_set")
        rstd_set = sem("rstd_set")
        offset_set = sem("offset_set")
        xn_set = sem("xn_set")
        q_dot_set = sem("q_dot_set")
        xbv_set = sem("xbv_set")
        top_set = sem("top_set")
        top_r_set = sem("top_r_set")
        shift_set = sem("shift_set")
        p_set = sem("p_set")
        inv_set = sem("inv_set")
        x1_set = sem("x1_set")
        stats1_set = sem("stats1_set")
        mean1_set = sem("mean1_set")
        eps1_set = sem("eps1_set")
        minus_mean1_set = sem("minus_mean1_set")
        rstd1_set = sem("rstd1_set")
        offset1_set = sem("offset1_set")
        xn1_set = sem("xn1_set")
        x1b_set = sem("x1b_set")
        y_set = sem("y_set")

        def count(b, j):
            return b * NT + (j + 1)

        def tile(j):
            return slice(j * P, (j + 1) * P)

        def full(t):
            return t.bitcast(F32)

        def spread(bank_):
            return bank_[:, :].rearrange("p (c q) -> p c q", c=NT)

        def every_batch(engine, step):
            step(0, 0, first=True)
            with engine.Fori(0, B // 2 - 1) as t:
                step(t, 1)
                step(t + 1, 0)
            step(B // 2 - 1, 1, last=True)

        def attention_order(of_v, of_scores, of_transposes, of_output):
            for j in range(NT - 1):
                of_v(j)
                of_scores(j)
            of_v(NT - 1)
            of_transposes(0)
            of_scores(NT - 1)
            of_transposes(1)
            for j in range(NT):
                of_output(j)
                if j + 2 < NT:
                    of_transposes(j + 2)

        block = stack.enter_context(nc.Block())

        @block.sync
        def _(sp):
            for c in range(NT):
                sp.dma_start(wq_raw[:, c, :], wq[tile(c), :]).then_inc(wqk_in[c], DMA)
                sp.dma_start(wk_raw[:, c, :], wk[tile(c), :]).then_inc(wqk_in[c], DMA)
            for j in range(NT):
                sp.dma_start(x_sb[:, 0, j, :], x[0, tile(j), :]).then_inc(x_in[j], DMA)
            sp.dma_start(bq_col[:, :], bq).then_inc(small_in, DMA)
            sp.dma_start(bk_col[:, :], bk).then_inc(small_in, DMA)
            sp.dma_start(ldT_sb[:, :], lora_downT).then_inc(lora_in, DMA)
            sp.dma_start(luT_sb[:, :], lora_upT).then_inc(lora_in, DMA)
            sp.dma_start(down_sb[:, :], down_aux).then_inc(lora_in, DMA)
            sp.dma_start(up_sb[:, :], up_auxT).then_inc(lora_in, DMA)
            sp.dma_start(ctx_raw[:, :, :], ctxT[0].rearrange("(c p) s -> p c s", p=P)).then_inc(ctx_in, DMA)
            sp.dma_start(wvT_raw[:, :, :], wvT.rearrange("(c p) e -> p c e", p=P)).then_inc(wv_in, DMA)
            sp.dma_start(bv_rows[:, :], bv).then_inc(bias_in, DMA)
            sp.dma_start(b_rows[:, :], b_ffn).then_inc(bias_in, DMA)
            sp.dma_start(wfT_raw[:, :, :], wT.rearrange("(c p) e -> p c e", p=P)).then_inc(wf_in, DMA)

            def step(half, odd, first=False, last=False):
                b = half * 2 + odd
                if first:
                    sp.wait_ge(vec_done, 2)
                for j in range(NT):
                    if not first:
                        sp.wait_ge(y_set, count(b - 1, j))
                        sp.dma_start(out[b - 1, tile(j), :], y_sb[:, j % 2, :]).then_inc(y_out[j % 2], DMA)
                    if not last:
                        sp.dma_start(x_sb[:, 1 - odd, j, :], x[b + 1, tile(j), :]).then_inc(x_in[j], DMA)
                if not last:
                    sp.wait_ge(ctx_lo_set, count(b, NT - 1))
                    sp.dma_start(ctx_raw[:, :, :], ctxT[b + 1].rearrange("(c p) s -> p c s", p=P)
                                 ).then_inc(ctx_in, DMA)

            every_batch(sp, step)
            for j in range(NT):
                sp.wait_ge(y_set, count(B - 1, j))
                sp.dma_start(out[B - 1, tile(j), :], y_sb[:, j % 2, :]).then_inc(y_out[j % 2], DMA)
            for k in range(2):
                sp.wait_ge(y_out[k], DMA * (1 + B * NT // 2))

        @block.scalar
        def _(act):
            def hi_of_x(b, j):
                act.wait_ge(xnT_done, count(b, j))
                act.activation(xnT_hi[:, :, tile(j)], spread(bank_t[1]), ACT.Identity).then_inc(xnT_hi_set, 1)

            def hi_of_ctx(b, j):
                if j == 0:
                    act.wait_ge(ctx_in, (b + 1) * DMA)
                act.activation(ctx_hi[:, j, :], ctx_raw[:, j, :], ACT.Identity).then_inc(ctx_hi_set, 1)

            def norm_of_x(b, odd, j):
                act.wait_ge(offset_set, count(b, j))
                act.activation(xn[:, j, :], x_sb[:, odd, j, :], ACT.Identity, bias=offset[:, j:j + 1],
                               scale=rstd[:, j:j + 1]).then_inc(xn_set, 1)

            for j in range(NT):
                norm_of_x(0, 0, j)
            for c in range(NT):
                act.wait_ge(m_done, c + 1)
                act.activation(m_hi[:, c, :], bank_m[c][:, :], ACT.Identity).then_inc(m_hi_set, 1)
            for j in range(NT):
                hi_of_x(0, j)
            act.wait_ge(wv_in, DMA)
            for c in range(NT):
                act.activation(wv_hi[:, c, :], wvT_raw[:, c, :], ACT.Identity).then_inc(wv_hi_set, 1)
            act.wait_ge(vec_set, 2)

            def step(half, odd, first=False, last=False):
                b = half * 2 + odd

                def hi_of_g(j):
                    act.wait_ge(g_done, count(b, j))
                    act.activation(gT_hi[:, j, :], bank_gv[j % 2][:, :], ACT.Identity,
                                   bias=g_bias[:, j:j + 1]).then_inc(g_hi_set, 1)

                def hi_of_x1(j):
                    act.wait_ge(xn1T_done, count(b - 1, j))
                    act.activation(rowT_hi[:, j, :, :], spread(bank_t[j % 2]), ACT.Identity
                                   ).then_inc(xn1T_hi_set, 1)

                def hi_of_v(j):
                    act.wait_ge(v_done, count(b, j))
                    act.activation(v_hi[:, j, :], bank_gv[j % 2][:, :], ACT.Identity).then_inc(v_hi_set, 1)

                def probabilities(j):
                    act.wait_ge(shift_set, count(b, j))
                    act.activation(row[:, j, :], bank_s[j % 2][:, :], ACT.Exp, bias=shift[:, j:j + 1],
                                   accum_out=row_sum[:, j:j + 1]).then_inc(p_set, 1)
                    if not last:
                        for i in {1: (0, 1), 2: (2,), 3: (3,)}.get(j, ()):
                            norm_of_x(b + 1, 1 - odd, i)

                def hi_of_p_and_x(j):
                    act.wait_ge(pT_done, count(b, j))
                    act.activation(rowT_hi[:, j, :, :], spread(bank_t[0]), ACT.Identity).then_inc(pT_hi_set, 1)
                    if not last:
                        hi_of_x(b + 1, j)

                def norm_of_x1(j):
                    act.wait_ge(offset1_set, count(b, j))
                    act.activation(row[:, j, :], x_sb[:, odd, j, :], ACT.Identity, bias=offset1[:, j:j + 1],
                                   scale=rstd1[:, j:j + 1]).then_inc(xn1_set, 1)

                hi_of_g(0)
                hi_of_g(1)
                if not first:
                    hi_of_x1(0)
                    hi_of_x1(1)
                hi_of_g(2)
                if not first:
                    hi_of_x1(2)
                    hi_of_x1(3)
                hi_of_g(3)
                if not first:
                    act.wait_ge(s_done, count(b - 1, NT - 1))
                for j in range(NT):
                    hi_of_ctx(b, j)
                if first:
                    for c in range(NT):
                        act.wait_ge(wf_sum, c + 1)
                        act.activation(wf_hi[:, c, :], wfT_raw[:, c, :], ACT.Identity).then_inc(wf_hi_set, 1)
                def of_scores(j):
                    if j < NT - 1:
                        probabilities(j)

                def of_transposes(j):
                    hi_of_p_and_x(j)
                    if j == 1:
                        probabilities(NT - 1)

                def of_output(j):
                    if j:
                        norm_of_x1(j - 1)

                attention_order(hi_of_v, of_scores, of_transposes, of_output)
                norm_of_x1(NT - 1)

            every_batch(act, step)
            for j in range(NT):
                act.wait_ge(xn1T_done, count(B - 1, j))
                act.activation(rowT_hi[:, j, :, :], spread(bank_t[j % 2]), ACT.Identity).then_inc(xn1T_hi_set, 1)

        @block.gpsimd
        def _(pool):
            pool.memset(ident[:, :], 0.0).then_inc(ident_set, 1)
            pool.wait_ge(ident_set, 1)
            pool.affine_select(out=ident[:, :], in_=ident[:, :], compare_op=ALU.not_equal, fill=1.0, base=0,
                               pattern=[[-1, P]], channel_multiplier=1).then_inc(ident_set, 1)
            pool.memset(minus_half[:, :], -0.5).then_inc(half_set, 1)
            pool.wait_ge(half_set, 1)

            def rstd_of_x(b, j):
                pool.wait_ge(eps_set, count(b, j))
                pool.tensor_tensor(rstd[:, j:j + 1], var_eps[:, j:j + 1], minus_half[:, :], ALU.pow
                                   ).then_inc(rstd_set, 1)
                pool.wait_ge(rstd_set, count(b, j))
                pool.wait_ge(minus_mean_set, count(b, j))
                pool.tensor_tensor(offset[:, j:j + 1], minus_mean[:, j:j + 1], rstd[:, j:j + 1], ALU.mult
                                   ).then_inc(offset_set, 1)

            def add_bv(b, odd, j):
                pool.wait_ge(xn_set, count(b, j))
                pool.tensor_tensor(x_sb[:, odd, j, :], x_sb[:, odd, j, :], bv_rows[:, :], ALU.add
                                   ).then_inc(xbv_set, 1)

            def rows_of_x(b, odd):
                for j in range(NT):
                    rstd_of_x(b, j)
                    if j:
                        add_bv(b, odd, j - 1)
                add_bv(b, odd, NT - 1)

            pool.wait_ge(bias_in, 2 * DMA)
            rows_of_x(0, 0)

            def step(half, odd, first=False, last=False):
                b = half * 2 + odd

                def rstd_of_x1(j):
                    pool.wait_ge(eps1_set, count(b, j))
                    pool.tensor_tensor(rstd1[:, j:j + 1], var_eps1[:, j:j + 1], minus_half[:, :], ALU.pow
                                       ).then_inc(rstd1_set, 1)
                    pool.wait_ge(rstd1_set, count(b, j))
                    pool.wait_ge(minus_mean1_set, count(b, j))
                    pool.tensor_tensor(offset1[:, j:j + 1], minus_mean1[:, j:j + 1], rstd1[:, j:j + 1], ALU.mult
                                       ).then_inc(offset1_set, 1)

                def add_b(j):
                    pool.wait_ge(xn1_set, count(b, j))
                    pool.tensor_tensor(x_sb[:, odd, j, :], x_sb[:, odd, j, :], b_rows[:, :], ALU.add
                                       ).then_inc(x1b_set, 1)

                for j in range(NT):
                    pool.wait_ge(ctx_hi_set, count(b, j))
                    pool.tensor_tensor(ctx_lo[:, j, :], ctx_raw[:, j, :], full(ctx_hi[:, j, :]), ALU.subtract
                                       ).then_inc(ctx_lo_set, 1)
                if not last:
                    rows_of_x(b + 1, 1 - odd)
                for j in range(NT):
                    rstd_of_x1(j)
                    if j:
                        add_b(j - 1)
                add_b(NT - 1)

            every_batch(pool, step)

        @block.vector
        def _(dve):
            dve.memset(zeros[:, :], 0.0).then_inc(zeros_set, 1)
            dve.wait_ge(zeros_set, 1)
            for k in range(2):
                dve.sem_inc(y_out[k], DMA)
            def lo_of(lo, whole, hi, done):
                dve.tensor_tensor(lo, whole, full(hi), ALU.subtract).then_inc(done, 1)

            def aggregation_waits(written, value):
                dve.wait_ge(written, value)
                dve.sem_inc(stats_seen, 1)

            def stats_of_x(b, odd, j):
                dve.wait_ge(x_in[j], (b + 1) * DMA)
                dve.bn_stats(stats[:, j, :], x_sb[:, odd, j, :]).then_inc(stats_set, 1)
                aggregation_waits(stats_set, count(b, j))
                dve.bn_aggr(mean_var[:, j, :], stats[:, j, :]).then_inc(mean_set, 1)
                dve.wait_ge(mean_set, count(b, j))
                dve.tensor_scalar(var_eps[:, j:j + 1], mean_var[:, j, 1:2], EPS, None, ALU.add
                                  ).then_inc(eps_set, 1)
                dve.tensor_scalar(minus_mean[:, j:j + 1], mean_var[:, j, 0:1], -1.0, None, ALU.mult
                                  ).then_inc(minus_mean_set, 1)

            def q_dot_bk_of_x(b, odd, j):
                dve.wait_ge(xn_set, count(b, j))
                if j:
                    dve.wait_ge(q_dot_set, count(b, j - 1))
                elif not (isinstance(b, int) and b == 0):
                    dve.wait_ge(q_dot_set, count(b - 1, NT - 1))
                dve.tensor_tensor_reduce(dots[:, :], xn[:, j, :], u_rows[:, :], 1.0, bqbk[:, :], ALU.mult,
                                         ALU.add, q_dot_bk[:, odd, j:j + 1]).then_inc(q_dot_set, 1)

            def lo_of_x(b, j):
                dve.wait_ge(xnT_hi_set, count(b, j))
                lo_of(xnT_lo[:, :, tile(j)], spread(bank_t[1]), xnT_hi[:, :, tile(j)], xnT_lo_set)

            for j in range(NT):
                stats_of_x(0, 0, j)
            dve.wait_ge(small_in, 2 * DMA)
            for c in range(NT):
                dve.tensor_scalar(bk_wide[:, c, :], zeros[:, :], bk_col[:, c:c + 1], None, ALU.add
                                  ).then_inc(bk_spread, 1)

            for c in range(NT):
                dve.wait_ge(m_hi_set, c + 1)
                lo_of(m_lo[:, c, :], bank_m[c][:, :], m_hi[:, c, :], m_lo_set)
            dve.wait_ge(t_done, 1)
            dve.tensor_copy(t1_sb, bank_s[0][0:RANK, :]).then_inc(t_set, 1)
            dve.wait_ge(vec_done, 1)
            dve.tensor_copy(g_bias[:, :], bank_s[1][:, 0:NT]).then_inc(vec_set, 1)
            dve.tensor_copy(bqbk[:, :], bank_s[1][:, NT:NT + 1]).then_inc(vec_set, 1)
            for j in range(NT):
                lo_of_x(0, j)
            dve.wait_ge(t_done, 2)
            dve.tensor_copy(t2_sb, bank_s[0][0:UDIM, :]).then_inc(t_set, 1)
            for c in range(NT):
                dve.wait_ge(wv_hi_set, c + 1)
                lo_of(wv_lo[:, c, :], wvT_raw[:, c, :], wv_hi[:, c, :], wv_lo_set)

            def u_and_wf():
                dve.wait_ge(vec_done, 2)
                dve.tensor_copy(u_rows[:, :], bank_s[0][:, :]).then_inc(vec_set, 1)
                dve.wait_ge(vec_set, 3)
                dve.wait_ge(wf_in, DMA)
                for c in range(NT):
                    dve.wait_ge(wf_done, c + 1)
                    dve.tensor_tensor(wfT_raw[:, c, :], bank_af[c % 2][:, :], wfT_raw[:, c, :], ALU.add
                                      ).then_inc(wf_sum, 1)
                for c in range(NT):
                    dve.wait_ge(wf_hi_set, c + 1)
                    lo_of(wf_lo[:, c, :], wfT_raw[:, c, :], wf_hi[:, c, :], wf_lo_set)

            def step(half, odd, first=False, last=False):
                b = half * 2 + odd

                def lo_of_g(j):
                    dve.wait_ge(g_hi_set, count(b, j))
                    dve.scalar_tensor_tensor(gT_lo[:, j, :], bank_gv[j % 2][:, :], g_bias[:, j:j + 1],
                                             full(gT_hi[:, j, :]), ALU.add, ALU.subtract
                                             ).then_inc(g_lo_set, 1)

                def lo_of_x1(j):
                    dve.wait_ge(xn1T_hi_set, count(b - 1, j))
                    lo_of(rowT_lo[:, j, :, :], spread(bank_t[j % 2]), rowT_hi[:, j, :, :], xn1T_lo_set)

                def lo_of_v(j):
                    dve.wait_ge(v_hi_set, count(b, j))
                    lo_of(v_lo[:, j, :], bank_gv[j % 2][:, :], v_hi[:, j, :], v_lo_set)

                def maximum(j):
                    dve.wait_ge(s_done, count(b, j))
                    dve.tensor_reduce(top[:, j:j + 1], bank_s[j % 2][:, :], AX_X, ALU.max).then_inc(top_set, 1)
                    dve.wait_ge(top_set, count(b, j))
                    dve.wait_ge(q_dot_set, count(b, j))
                    dve.tensor_tensor(top_r[:, j:j + 1], top[:, j:j + 1], q_dot_bk[:, odd, j:j + 1], ALU.add
                                      ).then_inc(top_r_set, 1)
                    dve.wait_ge(top_r_set, count(b, j))
                    dve.tensor_tensor(shift[:, j:j + 1], q_dot_bk[:, odd, j:j + 1], top_r[:, j:j + 1],
                                      ALU.subtract).then_inc(shift_set, 1)
                    if not last:
                        for i in {0: (0, 1), 1: (2,), 2: (3,)}.get(j, ()):
                            stats_of_x(b + 1, 1 - odd, i)

                def lo_of_p_and_x(j):
                    dve.wait_ge(pT_hi_set, count(b, j))
                    lo_of(rowT_lo[:, j, :, :], spread(bank_t[0]), rowT_hi[:, j, :, :], pT_lo_set)
                    if not last:
                        lo_of_x(b + 1, j)

                def x1_and_its_stats(j):
                    dve.wait_ge(p_set, count(b, j))
                    dve.reciprocal(inv_sum[:, j:j + 1], row_sum[:, j:j + 1]).then_inc(inv_set, 1)
                    dve.wait_ge(inv_set, count(b, j))
                    dve.wait_ge(a_done, count(b, j))
                    dve.wait_ge(xbv_set, count(b, j))
                    dve.scalar_tensor_tensor(x_sb[:, odd, j, :], bank_af[j % 2][:, :], inv_sum[:, j:j + 1],
                                             x_sb[:, odd, j, :], ALU.mult, ALU.add).then_inc(x1_set, 1)
                    dve.wait_ge(x1_set, count(b, j))
                    dve.bn_stats(stats1[:, j, :], x_sb[:, odd, j, :]).then_inc(stats1_set, 1)
                    aggregation_waits(stats1_set, count(b, j))
                    dve.bn_aggr(mean_var1[:, j, :], stats1[:, j, :]).then_inc(mean1_set, 1)
                    dve.wait_ge(mean1_set, count(b, j))
                    dve.tensor_scalar(var_eps1[:, j:j + 1], mean_var1[:, j, 1:2], EPS, None, ALU.add
                                      ).then_inc(eps1_set, 1)
                    dve.tensor_scalar(minus_mean1[:, j:j + 1], mean_var1[:, j, 0:1], -1.0, None, ALU.mult
                                      ).then_inc(minus_mean1_set, 1)

                if first:
                    dve.wait_ge(vec_set, 2)
                lo_of_g(0)
                lo_of_g(1)
                if not first:
                    lo_of_x1(0)
                    lo_of_x1(1)
                lo_of_g(2)
                if not first:
                    lo_of_x1(2)
                    lo_of_x1(3)
                lo_of_g(3)
                if first:
                    u_and_wf()
                for j in range(NT):
                    if not first:
                        y_of(1 - odd, b - 1, j)
                    q_dot_bk_of_x(b, odd, j)
                attention_order(lo_of_v, maximum, lo_of_p_and_x, x1_and_its_stats)

            def y_of(odd, b, j):
                dve.wait_ge(f_done, count(b, j))
                dve.wait_ge(x1b_set, count(b, j))
                dve.wait_ge(y_out[j % 2], (b * 2 + (1 + j // 2)) * DMA)
                dve.tensor_tensor(y_sb[:, j % 2, :], bank_af[j % 2][:, :], x_sb[:, odd, j, :], ALU.add
                                  ).then_inc(y_set, 1)

            every_batch(dve, step)
            for j in range(NT):
                dve.wait_ge(xn1T_hi_set, count(B - 1, j))
                lo_of(rowT_lo[:, j, :, :], spread(bank_t[j % 2]), rowT_hi[:, j, :, :], xn1T_lo_set)
            for j in range(NT):
                y_of(1, B - 1, j)

        @block.tensor
        def _(pe):
            def product(bank_, left, right, done):
                for c in range(NT):
                    (l_hi, l_lo), (r_hi, r_lo) = left(c), right(c)
                    pe.matmul(bank_[:, :], l_hi, r_hi, start=(c == 0), stop=False)
                    pe.matmul(bank_[:, :], l_hi, r_lo, start=False, stop=False)
                    last = pe.matmul(bank_[:, :], l_lo, r_hi, start=False, stop=(c == NT - 1))
                last.then_inc(done, 1)

            def transposes(bank_, source, done):
                for c in range(NT):
                    last = pe.transpose(bank_[:, tile(c)], source[:, tile(c)], ident[:, :])
                last.then_inc(done, 1)

            def transpose_x(b, j):
                pe.wait_ge(xn_set, count(b, j))
                if j:
                    pe.wait_ge(xnT_lo_set, count(b, j - 1))
                transposes(bank_t[1], xn[:, j, :], xnT_done)

            def transpose_x1(b, j):
                pe.wait_ge(xn1_set, count(b, j))
                transposes(bank_t[j % 2], row[:, j, :], xn1T_done)

            def ffn(b, j):
                pe.wait_ge(xn1T_lo_set, count(b, j))
                product(bank_af[j % 2], lambda c: (rowT_hi[:, j, c, :], rowT_lo[:, j, c, :]),
                        lambda c: (wf_hi[:, c, :], wf_lo[:, c, :]), f_done)

            for e in range(NT):
                pe.wait_ge(wqk_in[e], 2 * DMA)
                for c in range(NT):
                    last = pe.matmul(bank_m[c][:, :], wq_raw[:, e, tile(c)], wk_raw[:, e, :],
                                     start=(e == 0), stop=(e == NT - 1))
                    if e == NT - 1:
                        last.then_inc(m_done, 1)
            pe.wait_ge(lora_in, 4 * DMA)
            pe.matmul(bank_s[0][0:RANK, :], ldT_sb[:, :], down_sb[:, :], start=True, stop=True).then_inc(t_done, 1)
            pe.wait_ge(bk_spread, NT)
            for c in range(NT + 1):
                for e in range(NT):
                    left = wk_raw[:, e, tile(c)] if c < NT else bk_wide[:, e, :]
                    last = pe.matmul(bank_s[1][:, c:c + 1], left, bq_col[:, e:e + 1], start=(e == 0), stop=(e == NT - 1))
            last.then_inc(vec_done, 1)
            pe.wait_ge(ident_set, 2)
            for j in range(NT):
                transpose_x(0, j)
            pe.wait_ge(t_set, 1)
            pe.matmul(bank_s[0][0:UDIM, :], luT_sb[:, :], t1_sb, start=True, stop=True).then_inc(t_done, 1)

            def u_and_wf():
                pe.wait_ge(t_set, 2)
                for e in range(NT):
                    last = pe.matmul(bank_s[0][:, :], bk_wide[:, e, :], wq_raw[:, e, :],
                                     start=(e == 0), stop=(e == NT - 1))
                last.then_inc(vec_done, 1)
                for c in range(NT):
                    if c >= 2:
                        pe.wait_ge(wf_sum, c - 1)
                    pe.matmul(bank_af[c % 2][:, :], t2_sb[:, tile(c)], up_sb[:, :], start=True, stop=True
                              ).then_inc(wf_done, 1)

            def step(half, odd, first=False, last=False):
                b = half * 2 + odd

                def g(j):
                    if j >= 2:
                        pe.wait_ge(g_lo_set, count(b, j - 2))
                    elif not first:
                        pe.wait_ge(v_lo_set, count(b - 1, j + 2))
                    elif j == 0:
                        pe.wait_ge(m_lo_set, NT)
                    if j == 0:
                        pe.wait_ge(xnT_lo_set, count(b, NT - 1))
                    product(bank_gv[j % 2], lambda c: (m_hi[:, c, tile(j)], m_lo[:, c, tile(j)]),
                            lambda c: (xnT_hi[:, c, :], xnT_lo[:, c, :]), g_done)

                def x1T(j):
                    if first:
                        return
                    if j == 0:
                        pe.wait_ge(pT_lo_set, count(b - 1, NT - 1))
                    elif j == 1:
                        pe.wait_ge(xnT_lo_set, count(b, NT - 1))
                    else:
                        pe.wait_ge(xn1T_lo_set, count(b - 1, j - 2))
                    transpose_x1(b - 1, j)

                g(0)
                g(1)
                x1T(0)
                x1T(1)
                g(2)
                x1T(2)
                x1T(3)
                g(3)
                if not first:
                    for j in range(NT):
                        if j < 2:
                            pe.wait_ge(x1_set, count(b - 1, j + 2))
                        else:
                            pe.wait_ge(y_set, count(b - 1, j - 2))
                        ffn(b - 1, j)
                def v(j):
                    if j == 0:
                        pe.wait_ge(ctx_lo_set, count(b, NT - 1))
                        if first:
                            pe.wait_ge(wv_lo_set, NT)
                    if j < 2:
                        pe.wait_ge(g_lo_set, count(b, j + 2))
                    else:
                        pe.wait_ge(v_lo_set, count(b, j - 2))
                    product(bank_gv[j % 2], lambda c: (ctx_hi[:, c, tile(j)], ctx_lo[:, c, tile(j)]),
                            lambda c: (wv_hi[:, c, :], wv_lo[:, c, :]), v_done)

                def scores(j):
                    if j == 0:
                        pe.wait_ge(g_lo_set, count(b, NT - 1))
                        if first:
                            pe.wait_ge(vec_set, 3)
                    if j >= 2:
                        pe.wait_ge(p_set, count(b, j - 2))
                    elif not first:
                        pe.wait_ge(p_set, count(b - 1, j + 2))
                    product(bank_s[j % 2], lambda c: (gT_hi[:, c, tile(j)], gT_lo[:, c, tile(j)]),
                            lambda c: (ctx_hi[:, c, :], ctx_lo[:, c, :]), s_done)

                def pT_and_xT(j):
                    pe.wait_ge(p_set, count(b, j))
                    if j:
                        pe.wait_ge(pT_lo_set, count(b, j - 1))
                    elif not first:
                        pe.wait_ge(xn1T_lo_set, count(b - 1, 2))
                    transposes(bank_t[0], row[:, j, :], pT_done)
                    if not last:
                        if j == 0 and first:
                            pe.wait_ge(xnT_lo_set, NT)
                        elif j == 0:
                            pe.wait_ge(xn1T_lo_set, count(b - 1, 3))
                        transpose_x(b + 1, j)

                def output(j):
                    if j == 0:
                        pe.wait_ge(v_lo_set, count(b, NT - 1))
                        if first:
                            pe.wait_ge(wf_lo_set, NT)
                    pe.wait_ge(pT_lo_set, count(b, j))
                    if j >= 2:
                        pe.wait_ge(x1_set, count(b, j - 2))
                    elif not first:
                        pe.wait_ge(y_set, count(b - 1, j + 2))
                    product(bank_af[j % 2], lambda c: (rowT_hi[:, j, c, :], rowT_lo[:, j, c, :]),
                            lambda c: (v_hi[:, c, :], v_lo[:, c, :]), a_done)

                if first:
                    u_and_wf()
                attention_order(v, scores, pT_and_xT, output)

            every_batch(pe, step)

            def last_x1T(j):
                if j == 0:
                    pe.wait_ge(pT_lo_set, count(B - 1, NT - 1))
                elif j >= 2:
                    pe.wait_ge(xn1T_lo_set, count(B - 1, j - 2))
                transpose_x1(B - 1, j)

            def last_ffn(j):
                if j < 2:
                    pe.wait_ge(x1_set, count(B - 1, j + 2))
                else:
                    pe.wait_ge(y_set, count(B - 1, j - 2))
                ffn(B - 1, j)

            last_x1T(0)
            last_x1T(1)
            last_ffn(0)
            last_x1T(2)
            last_x1T(3)
            for j in range(1, NT):
                last_ffn(j)


_OUT = (32, 512, 512)


def kernel(x, ctx_1024, L0_xattn_Wq, L0_xattn_bq, L0_xattn_Wk, L0_xattn_bk, L0_xattn_Wv, L0_xattn_bv,
           L0_ffn_W, L0_ffn_b, L0_ffn_lora_down, L0_ffn_lora_up, L0_ffn_down_aux, L0_ffn_up_aux):
    import numpy as np
    import concourse.bacc as bacc
    from concourse.bass_utils import run_bass_kernel_spmd

    def column(v):
        return np.asarray(v).reshape(-1, P).T

    def rows(v):
        return np.broadcast_to(np.asarray(v), (P, v.shape[0]))

    def transposed(w):
        return np.swapaxes(np.asarray(w), -1, -2)

    layouts = {
        "x": x,
        "ctxT": transposed(ctx_1024),
        "wq": L0_xattn_Wq,
        "wk": L0_xattn_Wk,
        "wvT": transposed(L0_xattn_Wv),
        "wT": transposed(L0_ffn_W),
        "bq": column(L0_xattn_bq),
        "bk": column(L0_xattn_bk),
        "bv": rows(L0_xattn_bv),
        "b_ffn": rows(L0_ffn_b),
        "lora_downT": transposed(L0_ffn_lora_down),
        "lora_upT": transposed(L0_ffn_lora_up),
        "down_aux": L0_ffn_down_aux,
        "up_auxT": transposed(L0_ffn_up_aux),
    }
    nc = bacc.Bacc("TRN2", target_bir_lowering=False, num_devices=1)
    arrays, args = {}, []
    for name, value in layouts.items():
        a = np.ascontiguousarray(value)
        arrays[f"in_{name}"] = a
        args.append(nc.dram_tensor(f"in_{name}", a.shape, mybir.dt.from_np(a.dtype), kind="ExternalInput").ap())
    args.append(nc.dram_tensor("out_0", _OUT, F32, kind="ExternalOutput").ap())
    xattn_ffn_kernel(nc, *args)
    r = run_bass_kernel_spmd(nc, [arrays], core_ids=[0])
    return r.results[0]["out_0"]
```

```python
from contextlib import ExitStack

import concourse.bass as bass
from concourse import mybir
from concourse.alu_op_type import AluOpType as ALU

F32 = mybir.dt.float32
F32R = mybir.dt.float32r
ACT = mybir.ActivationFunctionType
AX_X = mybir.AxisListType.X

P = 128
EPS = 1e-5
WARMING_PRODUCTS = 12


def xattn_ffn_kernel(nc, x, xT, ctxT, wq, wk, wkT, wvT, wT, bq, bk_column, bk, bv, b_ffn,
                     lora_downT, lora_upT, down_aux, up_auxT, out):
    B, S, D = x.shape
    NT = D // P
    assert S == D == NT * P and B % 3 == 2 and B >= 5
    DDIM, RANK = lora_downT.shape
    UDIM = up_auxT.shape[0]
    DMA = 16

    with ExitStack() as stack:
        def sb(name, shape, dt=F32):
            return stack.enter_context(nc.sbuf_tensor(name, shape, dt))

        def pair(name, shape):
            return sb(name + "_hi", shape, F32R), sb(name + "_lo", shape, F32R)

        def bank(name):
            return stack.enter_context(nc.psum_tensor(name, [P, 512], F32))

        def sem(name):
            return stack.enter_context(nc.semaphore(name))

        m_hi, m_lo = pair("m", [P, NT, D])
        wv_hi, wv_lo = pair("wv", [P, NT, D])
        wf_hi, wf_lo = pair("wf", [P, NT, D])
        ctx_hi, ctx_lo = pair("ctx", [P, NT, S])
        xnT_hi, xnT_lo = pair("xnT", [P, NT, S])
        gT_hi, gT_lo = pair("gT", [P, NT, S])
        v_hi, v_lo = pair("v", [P, NT, D])
        rowT_hi, rowT_lo = pair("rowT", [P, NT, NT, P])

        x_sb = sb("x_sb", [P, 3, NT, D])
        ctx_raw = sb("ctx_raw", [P, NT, S])
        xT_raw = sb("xT_raw", [P, NT, S])
        ln_cols = sb("ln_cols", [P, 3, 2, NT])
        ln_rows = sb("ln_rows", [P, P, 2, NT])
        ln_dram = nc.dram_tensor("ln_stats", [P, 2, NT], F32, kind="Internal").ap()
        row = sb("row", [P, NT, D])
        y_sb = sb("y_sb", [P, 2, D])
        dots = sb("dots", [P, D])
        up_sb = dots[0:UDIM, :]

        bv_rows = sb("bv_rows", [P, D])
        b_rows = sb("b_rows", [P, D])
        wq_raw, wk_raw = x_sb[:, 1, :, :], x_sb[:, 2, :, :]
        wq_hi, wq_lo, wk_hi, wk_lo = gT_hi, gT_lo, v_hi, v_lo
        wvT_raw = wk_raw
        bq_rows, bk_rows = b_rows[:, :], bv_rows[:, :]
        wkT_raw = sb("wkT_raw", [P, NT, D])
        wfT_raw = row
        t1_sb = y_sb[0:RANK, 0, :]
        t2_sb = y_sb[0:UDIM, 1, :]
        ldT_sb = sb("ldT_sb", [DDIM, RANK])
        luT_sb = sb("luT_sb", [RANK, UDIM])
        bk_wide = sb("bk_wide", [P, NT, P])
        bk_col = sb("bk_col", [P, NT])
        u_rows = sb("u_rows", [P, D])
        down_sb = u_rows[0:DDIM, :]
        g_bias = sb("g_bias", [P, NT])
        bqbk = sb("bqbk", [P, 1])
        ident = sb("ident", [P, P])
        zeros = sb("zeros", [P, P])
        minus_half = sb("minus_half", [P, 1])

        stats = sb("stats", [P, NT, 6])
        mean_var = sb("mean_var", [P, NT, 2])
        var_eps = sb("var_eps", [P, NT])
        dot_u = sb("dot_u", [P, NT])
        sum_u = sb("sum_u", [P, 1])
        q_centred = sb("q_centred", [P, NT])
        q_scaled = sb("q_scaled", [P, NT])
        stats1 = sb("stats1", [P, NT, 6])
        mean_var1 = sb("mean_var1", [P, NT, 2])
        var_eps1 = sb("var_eps1", [P, NT])
        rstd1 = sb("rstd1", [P, NT])
        minus_mean1 = sb("minus_mean1", [P, NT])
        offset1 = sb("offset1", [P, NT])
        q_dot_bk = sb("q_dot_bk", [P, NT])
        top = sb("top", [P, NT])
        top_r = sb("top_r", [P, NT])
        shift = sb("shift", [P, NT])
        row_sum = sb("row_sum", [P, NT])
        inv_sum = sb("inv_sum", [P, NT])

        bank_gv = [bank("bank_gv0"), bank("bank_gv1")]
        bank_s = [bank("bank_s0"), bank("bank_s1")]
        bank_af = [bank("bank_af0"), bank("bank_af1")]
        bank_t = [bank("bank_t0"), bank("bank_t1")]

        bank_m = bank_gv + bank_af
        bank_wf = bank_af + bank_t

        wqk_in = [sem(f"wqk_in{c}") for c in range(NT)]
        wv_in = sem("wv_in")
        zeros_set = sem("zeros_set")
        bk_col_in = sem("bk_col_in")
        wkT_in = sem("wkT_in")
        lora_in = sem("lora_in")
        wf_in = sem("wf_in")
        bias_in = sem("bias_in")
        ident_set = sem("ident_set")
        half_set = sem("half_set")
        bk_spread = sem("bk_spread")
        wqk_hi_set = sem("wqk_hi_set")
        wqk_lo_set = [sem(f"wqk_lo_set{e}") for e in range(NT)]
        m_done = sem("m_done")
        m_hi_set = sem("m_hi_set")
        m_lo_set = sem("m_lo_set")
        bq_products = sem("bq_products")
        g_bias_set = sem("g_bias_set")
        u_done = sem("u_done")
        u_set = sem("u_set")
        t_done = sem("t_done")
        t_set = sem("t_set")
        wf_done = sem("wf_done")
        wf_sum = sem("wf_sum")
        wf_hi_set = sem("wf_hi_set")
        wf_lo_set = sem("wf_lo_set")
        wv_hi_set = sem("wv_hi_set")
        wv_lo_set = sem("wv_lo_set")

        ctx_in = sem("ctx_in")
        x_in = [sem(f"x_in{j}") for j in range(NT)]
        y_out = [sem(f"y_out{k}") for k in range(2)]

        g_done = sem("g_done")
        s_done = sem("s_done")
        v_done = sem("v_done")
        a_done = sem("a_done")
        f_done = sem("f_done")
        pT_done = sem("pT_done")
        xn1T_done = sem("xn1T_done")

        g_hi_set, g_lo_set = sem("g_hi_set"), sem("g_lo_set")
        v_hi_set, v_lo_set = sem("v_hi_set"), sem("v_lo_set")
        xnT_hi_set, xnT_lo_set = sem("xnT_hi_set"), sem("xnT_lo_set")
        pT_hi_set, pT_lo_set = sem("pT_hi_set"), sem("pT_lo_set")
        xn1T_hi_set, xn1T_lo_set = sem("xn1T_hi_set"), sem("xn1T_lo_set")
        ctx_hi_set, ctx_lo_set = sem("ctx_hi_set"), sem("ctx_lo_set")

        stats_set = sem("stats_set")
        mean_set = sem("mean_set")
        stats_seen = sem("stats_seen")
        eps_set = sem("eps_set")
        minus_mean_set = sem("minus_mean_set")
        ln_cols_set = sem("ln_cols_set")
        ln_out = sem("ln_out")
        ln_in = sem("ln_in")
        xT_in = sem("xT_in")
        first_centred_set = sem("first_centred_set")
        first_xn_set = sem("first_xn_set")
        centred_set = sem("centred_set")
        xn_set = sem("xn_set")
        dot_set = sem("dot_set")
        q_centred_set = sem("q_centred_set")
        q_scaled_set = sem("q_scaled_set")
        q_dot_set = sem("q_dot_set")
        xbv_set = sem("xbv_set")
        top_set = sem("top_set")
        top_r_set = sem("top_r_set")
        shift_set = sem("shift_set")
        p_set = sem("p_set")
        inv_set = sem("inv_set")
        x1_set = sem("x1_set")
        stats1_set = sem("stats1_set")
        mean1_set = sem("mean1_set")
        eps1_set = sem("eps1_set")
        minus_mean1_set = sem("minus_mean1_set")
        rstd1_set = sem("rstd1_set")
        offset1_set = sem("offset1_set")
        xn1_set = sem("xn1_set")
        x1b_set = sem("x1b_set")
        y_set = sem("y_set")

        def count(b, j):
            return b * NT + (j + 1)

        def norm_count(b, j):
            return count(b, j) - (NT - 1)

        def tile(j):
            return slice(j * P, (j + 1) * P)

        def columns(t, c):
            return t[:, c, :].rearrange("p (j q) -> p j q", j=NT)

        def ln_row(k):
            return ln_rows[:, :, k, :].rearrange("p q j -> p j q")

        def full(t):
            return t.bitcast(F32)

        def spread(bank_):
            return bank_[:, :].rearrange("p (c q) -> p c q", c=NT)

        def every_batch(engine, step):
            step(0, 0, first=True)
            with engine.Fori(0, B // 3) as t:
                step(t, 1)
                step(t, 2)
                step(t + 1, 0)
            step(B // 3, 1, last=True)

        def attention_order(of_v, of_scores, of_transposes, of_output):
            for j in range(NT - 1):
                of_v(j)
                of_scores(j)
            of_v(NT - 1)
            of_transposes(0)
            of_scores(NT - 1)
            of_transposes(1)
            for j in range(NT):
                of_output(j)
                if j + 2 < NT:
                    of_transposes(j + 2)

        block = stack.enter_context(nc.Block())

        @block.sync
        def _(sp):
            def load_x(b, slot, j):
                sp.dma_start(x_sb[:, slot, j, :], x[b, tile(j), :]).then_inc(x_in[j], DMA)

            def load_wqk(c):
                sp.dma_start(wq_raw[:, c, :], wq[tile(c), :]).then_inc(wqk_in[c], DMA)
                sp.dma_start(wk_raw[:, c, :], wk[tile(c), :]).then_inc(wqk_in[c], DMA)

            def ln_to_dram(b, slot):
                sp.wait_ge(ln_cols_set, b + 1)
                sp.dma_start(ln_dram, ln_cols[:, slot, :, :]).then_inc(ln_out, DMA)

            def ln_to_rows(b):
                sp.wait_ge(ln_out, (b + 1) * DMA)
                sp.dma_start(ln_rows[:, :, :, :], ln_dram.partition_broadcast(P)).then_inc(ln_in, DMA)

            load_x(0, 0, 0)
            load_x(0, 0, 1)
            load_wqk(0)
            load_x(0, 0, 2)
            load_x(0, 0, 3)
            for c in range(1, NT):
                load_wqk(c)
            sp.dma_start(bk_col[:, :], bk_column).then_inc(bk_col_in, DMA)
            sp.dma_start(ldT_sb[:, :], lora_downT).then_inc(lora_in, DMA)
            sp.dma_start(luT_sb[:, :], lora_upT).then_inc(lora_in, DMA)
            sp.dma_start(down_sb, down_aux).then_inc(lora_in, DMA)
            sp.dma_start(up_sb, up_auxT).then_inc(lora_in, DMA)
            ln_to_dram(0, 0)
            sp.dma_start(xT_raw[:, :, :], xT[0].rearrange("(c p) s -> p c s", p=P)).then_inc(xT_in, DMA)
            ln_to_rows(0)
            sp.dma_start(bq_rows, bq).then_inc(wkT_in, DMA)
            sp.dma_start(bk_rows, bk).then_inc(wkT_in, DMA)
            sp.dma_start(wkT_raw[:, :, :], wkT.rearrange("(c p) e -> p c e", p=P)).then_inc(wkT_in, DMA)
            for e in range(NT):
                sp.wait_ge(wqk_lo_set[e], 2)
            sp.dma_start(wvT_raw[:, :, :], wvT.rearrange("(c p) e -> p c e", p=P)).then_inc(wv_in, DMA)
            sp.dma_start(ctx_raw[:, :, :], ctxT[0].rearrange("(c p) s -> p c s", p=P)).then_inc(ctx_in, DMA)
            sp.dma_start(wfT_raw[:, :, :], wT.rearrange("(c p) e -> p c e", p=P)).then_inc(wf_in, DMA)

            def step(third, slot, first=False, last=False):
                b = third * 3 + slot
                if first:
                    sp.wait_ge(u_done, 1)
                if not last:
                    for j in range(NT):
                        load_x(b + 1, (slot + 1) % 3, j)
                    sp.wait_ge(xnT_lo_set, count(b, NT - 1))
                    sp.dma_start(xT_raw[:, :, :], xT[b + 1].rearrange("(c p) s -> p c s", p=P)
                                 ).then_inc(xT_in, DMA)
                if first:
                    sp.wait_ge(g_bias_set, NT + 1)
                    sp.dma_start(bv_rows[:, :], bv).then_inc(bias_in, DMA)
                    sp.dma_start(b_rows[:, :], b_ffn).then_inc(bias_in, DMA)
                if not last:
                    ln_to_dram(b + 1, (slot + 1) % 3)
                for j in range(NT):
                    if not first:
                        sp.wait_ge(y_set, count(b - 1, j))
                        sp.dma_start(out[b - 1, tile(j), :], y_sb[:, j % 2, :]).then_inc(y_out[j % 2], DMA)
                    if j == 0 and not last:
                        ln_to_rows(b + 1)
                if not last:
                    sp.wait_ge(ctx_lo_set, count(b, NT - 1))
                    sp.dma_start(ctx_raw[:, :, :], ctxT[b + 1].rearrange("(c p) s -> p c s", p=P)
                                 ).then_inc(ctx_in, DMA)
                if first:
                    sp.wait_ge(wv_lo_set, NT)

            every_batch(sp, step)
            for j in range(NT):
                sp.wait_ge(y_set, count(B - 1, j))
                sp.dma_start(out[B - 1, tile(j), :], y_sb[:, j % 2, :]).then_inc(y_out[j % 2], DMA)
            for k in range(2):
                sp.wait_ge(y_out[k], DMA * (1 + B * NT // 2))

        @block.scalar
        def _(act):
            def hi_of_x(b, j):
                if isinstance(b, int) and b == 0 and j < NT - 1:
                    act.wait_ge(first_xn_set, j + 1)
                else:
                    act.wait_ge(xn_set, norm_count(b, j))
                act.activation(xnT_hi[:, j, :], xT_raw[:, j, :], ACT.Identity).then_inc(xnT_hi_set, 1)

            def hi_of_ctx(b, j):
                if j == 0:
                    act.wait_ge(ctx_in, (b + 1) * DMA)
                act.activation(ctx_hi[:, j, :], ctx_raw[:, j, :], ACT.Identity).then_inc(ctx_hi_set, 1)

            for e in range(NT):
                act.wait_ge(wqk_in[e], 2 * DMA)
                act.activation(wq_hi[:, e, :], wq_raw[:, e, :], ACT.Identity).then_inc(wqk_hi_set, 1)
                act.activation(wk_hi[:, e, :], wk_raw[:, e, :], ACT.Identity).then_inc(wqk_hi_set, 1)
            for c in range(NT):
                act.wait_ge(m_done, c + 1)
                act.activation(m_hi[:, c, :], bank_m[c][:, :], ACT.Identity).then_inc(m_hi_set, 1)
            act.wait_ge(t_done, 1)
            act.activation(t1_sb, bank_s[0][0:RANK, :], ACT.Identity).then_inc(t_set, 1)
            for j in range(NT):
                hi_of_x(0, j)
            act.wait_ge(t_done, 2)
            act.activation(t2_sb, bank_s[0][0:UDIM, :], ACT.Identity).then_inc(t_set, 1)
            for c in range(NT):
                act.wait_ge(bq_products, c + 1)
                act.activation(wkT_raw[:, c, :], wkT_raw[:, c, :], ACT.Identity, accum_out=g_bias[:, c:c + 1]
                               ).then_inc(g_bias_set, 1)
            act.wait_ge(bq_products, NT + 1)
            act.activation(bq_rows, bq_rows, ACT.Identity, accum_out=bqbk[:, :]).then_inc(g_bias_set, 1)
            act.wait_ge(g_bias_set, NT)

            def hi_of_x1(b, j):
                act.wait_ge(xn1T_done, count(b, j))
                act.activation(rowT_hi[:, j, :, :], spread(bank_t[j % 2]), ACT.Identity).then_inc(xn1T_hi_set, 1)

            def step(third, slot, first=False, last=False):
                b = third * 3 + slot

                def hi_of_g(j):
                    act.wait_ge(g_done, count(b, j))
                    act.activation(gT_hi[:, j, :], bank_gv[j % 2][:, :], ACT.Identity,
                                   bias=g_bias[:, j:j + 1]).then_inc(g_hi_set, 1)

                def hi_of_v(j):
                    act.wait_ge(v_done, count(b, j))
                    act.activation(v_hi[:, j, :], bank_gv[j % 2][:, :], ACT.Identity).then_inc(v_hi_set, 1)

                def probabilities(j):
                    act.wait_ge(shift_set, count(b, j))
                    act.activation(row[:, j, :], bank_s[j % 2][:, :], ACT.Exp, bias=shift[:, j:j + 1],
                                   accum_out=row_sum[:, j:j + 1]).then_inc(p_set, 1)

                def hi_of_p(j):
                    act.wait_ge(pT_done, count(b, j))
                    act.activation(rowT_hi[:, j, :, :], spread(bank_t[j % 2]), ACT.Identity
                                   ).then_inc(pT_hi_set, 1)

                def norm_of_x1(j):
                    act.wait_ge(offset1_set, count(b, j))
                    act.activation(row[:, j, :], x_sb[:, slot, j, :], ACT.Identity, bias=offset1[:, j:j + 1],
                                   scale=rstd1[:, j:j + 1]).then_inc(xn1_set, 1)

                hi_of_g(0)
                if first:
                    act.wait_ge(wv_in, DMA)
                    for c in range(NT):
                        act.activation(wv_hi[:, c, :], wvT_raw[:, c, :], ACT.Identity).then_inc(wv_hi_set, 1)
                hi_of_g(1)
                if first:
                    for j in range(NT):
                        hi_of_ctx(b, j)
                else:
                    hi_of_x1(b - 1, 0)
                    hi_of_x1(b - 1, 1)
                hi_of_g(2)
                if not first:
                    hi_of_x1(b - 1, 2)
                    hi_of_x1(b - 1, 3)
                hi_of_g(3)
                if not first:
                    act.wait_ge(s_done, count(b - 1, NT - 1))
                    for j in range(NT):
                        hi_of_ctx(b, j)
                if first:
                    for c in range(NT):
                        act.wait_ge(wf_sum, c + 1)
                        act.activation(wf_hi[:, c, :], wfT_raw[:, c, :], ACT.Identity).then_inc(wf_hi_set, 1)
                def of_v(j):
                    hi_of_v(j)
                    if j >= 2 and not last:
                        hi_of_x(b + 1, 2 * j - 3)

                def of_scores(j):
                    if j < NT - 1:
                        probabilities(j)
                    if 1 <= j < NT - 1 and not last:
                        hi_of_x(b + 1, 2 * j - 2)

                def of_transposes(j):
                    hi_of_p(j)
                    if j == 1:
                        probabilities(NT - 1)

                def of_output(j):
                    if j >= 2:
                        norm_of_x1(j - 2)

                attention_order(of_v, of_scores, of_transposes, of_output)
                if last:
                    hi_of_x1(b, 0)
                norm_of_x1(NT - 2)
                if last:
                    hi_of_x1(b, 1)
                norm_of_x1(NT - 1)

            every_batch(act, step)
            for j in range(2, NT):
                hi_of_x1(B - 1, j)

        @block.gpsimd
        def _(pool):
            pool.memset(ident[:, :], 0.0).then_inc(ident_set, 1)
            pool.wait_ge(ident_set, 1)
            pool.affine_select(out=ident[:, :], in_=ident[:, :], compare_op=ALU.not_equal, fill=1.0, base=0,
                               pattern=[[-1, P]], channel_multiplier=1).then_inc(ident_set, 1)
            def lo_of_wk(e):
                pool.wait_ge(wqk_hi_set, 2 * e + 2)
                pool.tensor_tensor(wk_lo[:, e, :], wk_raw[:, e, :], full(wk_hi[:, e, :]), ALU.subtract
                                   ).then_inc(wqk_lo_set[e], 1)

            pool.memset(minus_half[:, :], -0.5).then_inc(half_set, 1)
            pool.wait_ge(half_set, 1)

            def columns_of_x(b, slot):
                pool.wait_ge(eps_set, count(b, NT - 1))
                pool.wait_ge(minus_mean_set, count(b, NT - 1))
                if not (isinstance(b, int) and b <= 1):
                    pool.wait_ge(q_dot_set, b - 1)
                    pool.wait_ge(ln_out, (b - 1) * DMA)
                pool.tensor_tensor(ln_cols[:, slot, 0, :], var_eps[:, :], minus_half[:, :].to_broadcast([P, NT]),
                                   ALU.pow).then_inc(ln_cols_set, 1)

            def norm_of_x(b, tiles):
                pool.wait_ge(xT_in, (b + 1) * DMA)
                pool.wait_ge(ln_in, (b + 1) * DMA)
                for j in tiles:
                    pool.tensor_tensor(columns(xT_raw, j), columns(xT_raw, j), ln_row(1), ALU.add
                                       ).then_inc(centred_set, 1)
                    pool.wait_ge(centred_set, norm_count(b, j))
                    pool.tensor_tensor(columns(xT_raw, j), columns(xT_raw, j), ln_row(0), ALU.mult
                                       ).then_inc(xn_set, 1)

            lo_of_wk(0)
            columns_of_x(0, 0)
            lo_of_wk(1)
            norm_of_x(0, [NT - 1])
            pool.wait_ge(wkT_in, 3 * DMA)
            for c in range(NT):
                pool.tensor_tensor(wkT_raw[:, c, :], wkT_raw[:, c, :], bq_rows, ALU.mult).then_inc(bq_products, 1)
            pool.wait_ge(bq_products, NT)
            pool.tensor_tensor(bq_rows, bq_rows, bk_rows, ALU.mult).then_inc(bq_products, 1)

            def step(third, slot, first=False, last=False):
                b = third * 3 + slot

                def rstd_of_x1(j):
                    pool.wait_ge(eps1_set, count(b, j))
                    pool.tensor_tensor(rstd1[:, j:j + 1], var_eps1[:, j:j + 1], minus_half[:, :], ALU.pow
                                       ).then_inc(rstd1_set, 1)
                    pool.wait_ge(rstd1_set, count(b, j))
                    pool.wait_ge(minus_mean1_set, count(b, j))
                    pool.tensor_tensor(offset1[:, j:j + 1], minus_mean1[:, j:j + 1], rstd1[:, j:j + 1], ALU.mult
                                       ).then_inc(offset1_set, 1)

                def add_b(j):
                    pool.wait_ge(xn1_set, count(b, j))
                    pool.tensor_tensor(x_sb[:, slot, j, :], x_sb[:, slot, j, :], b_rows[:, :], ALU.add
                                       ).then_inc(x1b_set, 1)

                if not first and not last:
                    columns_of_x(b + 1, (slot + 1) % 3)
                for j in range(NT):
                    pool.wait_ge(ctx_hi_set, count(b, j))
                    pool.tensor_tensor(ctx_lo[:, j, :], ctx_raw[:, j, :], full(ctx_hi[:, j, :]), ALU.subtract
                                       ).then_inc(ctx_lo_set, 1)
                if first:
                    columns_of_x(b + 1, (slot + 1) % 3)
                if not last:
                    norm_of_x(b + 1, range(NT))
                if first:
                    pool.wait_ge(bias_in, 2 * DMA)
                for j in range(NT):
                    pool.wait_ge(dot_set, count(b, j))
                    pool.tensor_tensor(x_sb[:, slot, j, :], x_sb[:, slot, j, :], bv_rows[:, :], ALU.add
                                       ).then_inc(xbv_set, 1)
                for j in range(NT):
                    rstd_of_x1(j)
                    if j:
                        add_b(j - 1)
                add_b(NT - 1)

            every_batch(pool, step)

        @block.vector
        def _(dve):
            dve.memset(zeros[:, :], 0.0).then_inc(zeros_set, 1)
            dve.wait_ge(zeros_set, 1)
            for k in range(2):
                dve.sem_inc(y_out[k], DMA)
            def lo_of(lo, whole, hi, done):
                dve.tensor_tensor(lo, whole, full(hi), ALU.subtract).then_inc(done, 1)

            def aggregation_waits(written, value):
                dve.wait_ge(written, value)
                dve.sem_inc(stats_seen, 1)

            def stats_of_x(b, slot, j):
                dve.wait_ge(x_in[j], (b + 1) * DMA)
                dve.bn_stats(stats[:, j, :], x_sb[:, slot, j, :]).then_inc(stats_set, 1)
                aggregation_waits(stats_set, count(b, j))
                dve.bn_aggr(mean_var[:, j, :], stats[:, j, :]).then_inc(mean_set, 1)
                dve.wait_ge(mean_set, count(b, j))
                dve.tensor_scalar(var_eps[:, j:j + 1], mean_var[:, j, 1:2], EPS, None, ALU.add
                                  ).then_inc(eps_set, 1)
                dve.tensor_scalar(ln_cols[:, slot, 1, j:j + 1], mean_var[:, j, 0:1], -1.0, None, ALU.mult
                                  ).then_inc(minus_mean_set, 1)

            def dot_of_x(b, slot, j):
                if j:
                    dve.wait_ge(dot_set, count(b, j - 1))
                elif not (isinstance(b, int) and b == 0):
                    dve.wait_ge(dot_set, count(b - 1, NT - 1))
                dve.tensor_tensor_reduce(dots[:, :], x_sb[:, slot, j, :], u_rows[:, :], 1.0, 0.0, ALU.mult,
                                         ALU.add, dot_u[:, j:j + 1]).then_inc(dot_set, 1)

            def q_dot_bk_of(b, slot):
                dve.wait_ge(dot_set, count(b, NT - 1))
                dve.scalar_tensor_tensor(q_centred[:, :], ln_cols[:, slot, 1, :], sum_u[:, :], dot_u[:, :],
                                         ALU.mult, ALU.add).then_inc(q_centred_set, 1)
                dve.wait_ge(q_centred_set, b + 1)
                dve.wait_ge(ln_cols_set, b + 1)
                dve.tensor_tensor(q_scaled[:, :], q_centred[:, :], ln_cols[:, slot, 0, :], ALU.mult
                                  ).then_inc(q_scaled_set, 1)
                dve.wait_ge(q_scaled_set, b + 1)
                dve.tensor_scalar(q_dot_bk[:, :], q_scaled[:, :], bqbk[:, :], None, ALU.add
                                  ).then_inc(q_dot_set, 1)

            def lo_of_x(b, j):
                dve.wait_ge(xnT_hi_set, count(b, j))
                lo_of(xnT_lo[:, j, :], xT_raw[:, j, :], xnT_hi[:, j, :], xnT_lo_set)

            for e in range(NT):
                if e < 2:
                    stats_of_x(0, 0, 2 * e)
                    stats_of_x(0, 0, 2 * e + 1)
                dve.wait_ge(wqk_hi_set, 2 * e + 1)
                lo_of(wq_lo[:, e, :], wq_raw[:, e, :], wq_hi[:, e, :], wqk_lo_set[e])
                if e >= 2:
                    dve.wait_ge(wqk_hi_set, 2 * e + 2)
                    lo_of(wk_lo[:, e, :], wk_raw[:, e, :], wk_hi[:, e, :], wqk_lo_set[e])
            dve.wait_ge(bk_col_in, DMA)
            for c in range(NT):
                dve.tensor_scalar(bk_wide[:, c, :], zeros[:, :], bk_col[:, c:c + 1], None, ALU.add
                                  ).then_inc(bk_spread, 1)
            dve.wait_ge(xT_in, DMA)
            dve.wait_ge(ln_in, DMA)
            for j in range(NT - 1):
                dve.tensor_tensor(columns(xT_raw, j), columns(xT_raw, j), ln_row(1), ALU.add
                                  ).then_inc(first_centred_set, 1)
            for j in range(NT - 1):
                dve.wait_ge(first_centred_set, j + 1)
                dve.tensor_tensor(columns(xT_raw, j), columns(xT_raw, j), ln_row(0), ALU.mult
                                  ).then_inc(first_xn_set, 1)
            for c in range(NT):
                dve.wait_ge(m_hi_set, c + 1)
                lo_of(m_lo[:, c, :], bank_m[c][:, :], m_hi[:, c, :], m_lo_set)
            for j in range(NT):
                lo_of_x(0, j)
            dve.wait_ge(u_done, 1)
            dve.tensor_copy(u_rows[:, :], bank_s[1][:, :]).then_inc(u_set, 1)
            dve.tensor_reduce(sum_u[:, :], bank_s[1][:, :], AX_X, ALU.add).then_inc(u_set, 1)

            def wf_sums():
                dve.wait_ge(u_set, 2)
                dve.wait_ge(g_bias_set, NT + 1)
                dve.wait_ge(wf_in, DMA)
                for c in range(NT):
                    dve.wait_ge(wf_done, c + 1)
                    dve.tensor_tensor(wfT_raw[:, c, :], bank_wf[c][:, :], wfT_raw[:, c, :], ALU.add
                                      ).then_inc(wf_sum, 1)

            def split_of_wf():
                for c in range(NT):
                    dve.wait_ge(wf_hi_set, c + 1)
                    lo_of(wf_lo[:, c, :], wfT_raw[:, c, :], wf_hi[:, c, :], wf_lo_set)

            def lo_of_x1(b, j):
                dve.wait_ge(xn1T_hi_set, count(b, j))
                lo_of(rowT_lo[:, j, :, :], spread(bank_t[j % 2]), rowT_hi[:, j, :, :], xn1T_lo_set)

            def step(third, slot, first=False, last=False):
                b = third * 3 + slot

                def lo_of_g(j):
                    dve.wait_ge(g_hi_set, count(b, j))
                    dve.scalar_tensor_tensor(gT_lo[:, j, :], bank_gv[j % 2][:, :], g_bias[:, j:j + 1],
                                             full(gT_hi[:, j, :]), ALU.add, ALU.subtract
                                             ).then_inc(g_lo_set, 1)

                def lo_of_v(j):
                    dve.wait_ge(v_hi_set, count(b, j))
                    lo_of(v_lo[:, j, :], bank_gv[j % 2][:, :], v_hi[:, j, :], v_lo_set)
                    if j >= 2 and not last:
                        lo_of_x(b + 1, 2 * j - 3)

                def maximum(j):
                    dve.wait_ge(s_done, count(b, j))
                    dve.tensor_reduce(top[:, j:j + 1], bank_s[j % 2][:, :], AX_X, ALU.max).then_inc(top_set, 1)
                    dve.wait_ge(top_set, count(b, j))
                    dve.wait_ge(q_dot_set, b + 1)
                    dve.tensor_tensor(top_r[:, j:j + 1], top[:, j:j + 1], q_dot_bk[:, j:j + 1], ALU.add
                                      ).then_inc(top_r_set, 1)
                    dve.wait_ge(top_r_set, count(b, j))
                    dve.tensor_tensor(shift[:, j:j + 1], q_dot_bk[:, j:j + 1], top_r[:, j:j + 1],
                                      ALU.subtract).then_inc(shift_set, 1)
                    if 1 <= j < NT - 1 and not last:
                        lo_of_x(b + 1, 2 * j - 2)

                def lo_of_p(j):
                    dve.wait_ge(pT_hi_set, count(b, j))
                    lo_of(rowT_lo[:, j, :, :], spread(bank_t[j % 2]), rowT_hi[:, j, :, :], pT_lo_set)

                def inverse_sum(j):
                    dve.wait_ge(p_set, count(b, j))
                    dve.reciprocal(inv_sum[:, j:j + 1], row_sum[:, j:j + 1]).then_inc(inv_set, 1)

                def x1_and_its_stats(j):
                    if last and j == NT - 1:
                        lo_of_x1(b, 0)
                    dve.wait_ge(inv_set, count(b, j))
                    dve.wait_ge(a_done, count(b, j))
                    dve.wait_ge(xbv_set, count(b, j))
                    dve.scalar_tensor_tensor(x_sb[:, slot, j, :], bank_af[j % 2][:, :], inv_sum[:, j:j + 1],
                                             x_sb[:, slot, j, :], ALU.mult, ALU.add).then_inc(x1_set, 1)
                    dve.wait_ge(x1_set, count(b, j))
                    dve.bn_stats(stats1[:, j, :], x_sb[:, slot, j, :]).then_inc(stats1_set, 1)
                    if j + 2 < NT:
                        lo_of_p(j + 2)
                    aggregation_waits(stats1_set, count(b, j))
                    dve.bn_aggr(mean_var1[:, j, :], stats1[:, j, :]).then_inc(mean1_set, 1)
                    if j < NT - 1:
                        inverse_sum(j + 1)
                    dve.wait_ge(mean1_set, count(b, j))
                    dve.tensor_scalar(var_eps1[:, j:j + 1], mean_var1[:, j, 1:2], EPS, None, ALU.add
                                      ).then_inc(eps1_set, 1)
                    dve.tensor_scalar(minus_mean1[:, j:j + 1], mean_var1[:, j, 0:1], -1.0, None, ALU.mult
                                      ).then_inc(minus_mean1_set, 1)

                if first:
                    dve.wait_ge(g_bias_set, NT)
                def next_stats(*tiles):
                    if not last:
                        for j in tiles:
                            stats_of_x(b + 1, (slot + 1) % 3, j)

                lo_of_g(0)
                if first:
                    for c in range(NT):
                        dve.wait_ge(wv_hi_set, c + 1)
                        lo_of(wv_lo[:, c, :], wvT_raw[:, c, :], wv_hi[:, c, :], wv_lo_set)
                else:
                    next_stats(0)
                lo_of_g(1)
                if not first:
                    lo_of_x1(b - 1, 0)
                    lo_of_x1(b - 1, 1)
                    next_stats(1)
                lo_of_g(2)
                if first:
                    next_stats(0, 1)
                else:
                    lo_of_x1(b - 1, 2)
                    lo_of_x1(b - 1, 3)
                next_stats(2)
                lo_of_g(3)
                next_stats(3)
                if first:
                    wf_sums()
                for j in range(NT):
                    if not first:
                        y_of((slot + 2) % 3, b - 1, j)
                    dot_of_x(b, slot, j)
                q_dot_bk_of(b, slot)
                if first:
                    split_of_wf()
                def of_transposes(j):
                    if j < 2:
                        lo_of_p(j)
                    if j == 1:
                        inverse_sum(0)

                attention_order(lo_of_v, maximum, of_transposes, x1_and_its_stats)

            def y_of(slot, b, j):
                dve.wait_ge(f_done, count(b, j))
                dve.wait_ge(x1b_set, count(b, j))
                dve.wait_ge(y_out[j % 2], (b * 2 + (1 + j // 2)) * DMA)
                dve.tensor_tensor(y_sb[:, j % 2, :], bank_af[j % 2][:, :], x_sb[:, slot, j, :], ALU.add
                                  ).then_inc(y_set, 1)

            every_batch(dve, step)
            lo_of_x1(B - 1, 1)
            lo_of_x1(B - 1, 2)
            y_of(1, B - 1, 0)
            lo_of_x1(B - 1, 3)
            for j in range(1, NT):
                y_of(1, B - 1, j)

        @block.tensor
        def _(pe):
            def product(bank_, left, right, done):
                for c in range(NT):
                    (l_hi, l_lo), (r_hi, r_lo) = left(c), right(c)
                    pe.matmul(bank_[:, :], l_hi, r_hi, start=(c == 0), stop=False)
                    pe.matmul(bank_[:, :], l_hi, r_lo, start=False, stop=False)
                    last = pe.matmul(bank_[:, :], l_lo, r_hi, start=False, stop=(c == NT - 1))
                last.then_inc(done, 1)

            def transposes(bank_, source, done):
                for c in range(NT):
                    last = pe.transpose(bank_[:, tile(c)], source[:, tile(c)], ident[:, :])
                last.then_inc(done, 1)

            def transpose_x1(b, j):
                pe.wait_ge(xn1_set, count(b, j))
                transposes(bank_t[j % 2], row[:, j, :], xn1T_done)

            def ffn(b, j):
                pe.wait_ge(xn1T_lo_set, count(b, j))
                product(bank_af[j % 2], lambda c: (rowT_hi[:, j, c, :], rowT_lo[:, j, c, :]),
                        lambda c: (wf_hi[:, c, :], wf_lo[:, c, :]), f_done)

            pe.wait_ge(zeros_set, 1)
            for _ in range(WARMING_PRODUCTS):
                pe.matmul(bank_t[0][:, 0:P], zeros[:, :], zeros[:, :], start=True, stop=True)
            for e in range(NT):
                pe.wait_ge(wqk_hi_set, 2 * e + 2)
                pe.wait_ge(wqk_lo_set[e], 2)
                for c in range(NT):
                    pe.matmul(bank_m[c][:, :], wq_hi[:, e, tile(c)], wk_hi[:, e, :], start=(e == 0), stop=False)
                    pe.matmul(bank_m[c][:, :], wq_lo[:, e, tile(c)], wk_hi[:, e, :], start=False, stop=False)
                    last = pe.matmul(bank_m[c][:, :], wq_hi[:, e, tile(c)], wk_lo[:, e, :],
                                     start=False, stop=(e == NT - 1))
                    if e == NT - 1:
                        last.then_inc(m_done, 1)
            pe.wait_ge(lora_in, 4 * DMA)
            pe.matmul(bank_s[0][0:RANK, :], ldT_sb[:, :], down_sb, start=True, stop=True).then_inc(t_done, 1)
            pe.wait_ge(bk_spread, NT)
            for e in range(NT):
                last = pe.matmul(bank_s[1][:, :], bk_wide[:, e, :], wq_raw[:, e, :],
                                 start=(e == 0), stop=(e == NT - 1))
            last.then_inc(u_done, 1)
            pe.wait_ge(t_set, 1)
            pe.matmul(bank_s[0][0:UDIM, :], luT_sb[:, :], t1_sb, start=True, stop=True).then_inc(t_done, 1)
            pe.wait_ge(ident_set, 2)

            def last_x1T(j):
                if j < 2:
                    pe.wait_ge(pT_lo_set, count(B - 1, j + 2))
                else:
                    pe.wait_ge(xn1T_lo_set, count(B - 1, j - 2))
                transpose_x1(B - 1, j)

            def low_rank_wf():
                pe.wait_ge(t_set, 2)
                for c in range(NT):
                    pe.matmul(bank_wf[c][:, :], t2_sb[:, tile(c)], up_sb, start=True, stop=True
                              ).then_inc(wf_done, 1)

            def step(third, slot, first=False, last=False):
                b = third * 3 + slot

                def g(j):
                    if j >= 2:
                        pe.wait_ge(g_lo_set, count(b, j - 2))
                    elif not first:
                        pe.wait_ge(v_lo_set, count(b - 1, j + 2))
                    elif j == 0:
                        pe.wait_ge(m_lo_set, NT)
                    if j == 0:
                        pe.wait_ge(xnT_lo_set, count(b, NT - 1))
                    product(bank_gv[j % 2], lambda c: (m_hi[:, c, tile(j)], m_lo[:, c, tile(j)]),
                            lambda c: (xnT_hi[:, c, :], xnT_lo[:, c, :]), g_done)

                def x1T(j):
                    if first:
                        return
                    if j < 2:
                        pe.wait_ge(pT_lo_set, count(b - 1, j + 2))
                    else:
                        pe.wait_ge(xn1T_lo_set, count(b - 1, j - 2))
                    transpose_x1(b - 1, j)

                g(0)
                g(1)
                x1T(0)
                x1T(1)
                g(2)
                x1T(2)
                x1T(3)
                g(3)
                if not first:
                    for j in range(NT):
                        if j < 2:
                            pe.wait_ge(x1_set, count(b - 1, j + 2))
                        else:
                            pe.wait_ge(y_set, count(b - 1, j - 2))
                        ffn(b - 1, j)
                def v(j):
                    if j == 0:
                        pe.wait_ge(ctx_lo_set, count(b, NT - 1))
                        if first:
                            pe.wait_ge(wv_lo_set, NT)
                    if j < 2:
                        pe.wait_ge(g_lo_set, count(b, j + 2))
                    else:
                        pe.wait_ge(v_lo_set, count(b, j - 2))
                    product(bank_gv[j % 2], lambda c: (ctx_hi[:, c, tile(j)], ctx_lo[:, c, tile(j)]),
                            lambda c: (wv_hi[:, c, :], wv_lo[:, c, :]), v_done)

                def scores(j):
                    if j == 0:
                        pe.wait_ge(g_lo_set, count(b, NT - 1))
                        if first:
                            pe.wait_ge(t_set, 2)
                            pe.wait_ge(u_set, 2)
                    if j >= 2:
                        pe.wait_ge(p_set, count(b, j - 2))
                    elif not first:
                        pe.wait_ge(p_set, count(b - 1, j + 2))
                    product(bank_s[j % 2], lambda c: (gT_hi[:, c, tile(j)], gT_lo[:, c, tile(j)]),
                            lambda c: (ctx_hi[:, c, :], ctx_lo[:, c, :]), s_done)

                def pT(j):
                    pe.wait_ge(p_set, count(b, j))
                    if j >= 2:
                        pe.wait_ge(pT_lo_set, count(b, j - 2))
                    elif not first:
                        pe.wait_ge(xn1T_lo_set, count(b - 1, j + 2))
                    else:
                        pe.wait_ge(wf_sum, NT)
                    transposes(bank_t[j % 2], row[:, j, :], pT_done)

                def output(j):
                    if last and j == NT - 1:
                        last_x1T(0)
                    if j == 0:
                        pe.wait_ge(v_lo_set, count(b, NT - 1))
                        if first:
                            pe.wait_ge(wf_lo_set, NT)
                    pe.wait_ge(pT_lo_set, count(b, j))
                    if j >= 2:
                        pe.wait_ge(x1_set, count(b, j - 2))
                    elif not first:
                        pe.wait_ge(y_set, count(b - 1, j + 2))
                    product(bank_af[j % 2], lambda c: (rowT_hi[:, j, c, :], rowT_lo[:, j, c, :]),
                            lambda c: (v_hi[:, c, :], v_lo[:, c, :]), a_done)

                if first:
                    low_rank_wf()
                attention_order(v, scores, pT, output)

            def last_ffn(j):
                if j < 2:
                    pe.wait_ge(x1_set, count(B - 1, j + 2))
                else:
                    pe.wait_ge(y_set, count(B - 1, j - 2))
                ffn(B - 1, j)

            every_batch(pe, step)
            last_x1T(1)
            last_ffn(0)
            last_x1T(2)
            last_ffn(1)
            last_x1T(3)
            last_ffn(2)
            last_ffn(3)


_OUT = (32, 512, 512)


def kernel(x, ctx_1024, L0_xattn_Wq, L0_xattn_bq, L0_xattn_Wk, L0_xattn_bk, L0_xattn_Wv, L0_xattn_bv,
           L0_ffn_W, L0_ffn_b, L0_ffn_lora_down, L0_ffn_lora_up, L0_ffn_down_aux, L0_ffn_up_aux):
    import numpy as np
    import concourse.bacc as bacc
    from concourse.bass_utils import run_bass_kernel_spmd

    def column(v):
        return np.asarray(v).reshape(-1, P).T

    def rows(v):
        return np.broadcast_to(np.asarray(v), (P, v.shape[0]))

    def transposed(w):
        return np.swapaxes(np.asarray(w), -1, -2)

    layouts = {
        "x": x,
        "xT": transposed(x),
        "ctxT": transposed(ctx_1024),
        "wq": L0_xattn_Wq,
        "wk": L0_xattn_Wk,
        "wkT": transposed(L0_xattn_Wk),
        "wvT": transposed(L0_xattn_Wv),
        "wT": transposed(L0_ffn_W),
        "bq": rows(L0_xattn_bq),
        "bk_column": column(L0_xattn_bk),
        "bk": rows(L0_xattn_bk),
        "bv": rows(L0_xattn_bv),
        "b_ffn": rows(L0_ffn_b),
        "lora_downT": transposed(L0_ffn_lora_down),
        "lora_upT": transposed(L0_ffn_lora_up),
        "down_aux": L0_ffn_down_aux,
        "up_auxT": transposed(L0_ffn_up_aux),
    }
    nc = bacc.Bacc("TRN2", target_bir_lowering=False, num_devices=1)
    arrays, args = {}, []
    for name, value in layouts.items():
        a = np.ascontiguousarray(value)
        arrays[f"in_{name}"] = a
        args.append(nc.dram_tensor(f"in_{name}", a.shape, mybir.dt.from_np(a.dtype), kind="ExternalInput").ap())
    args.append(nc.dram_tensor("out_0", _OUT, F32, kind="ExternalOutput").ap())
    xattn_ffn_kernel(nc, *args)
    r = run_bass_kernel_spmd(nc, [arrays], core_ids=[0])
    return r.results[0]["out_0"]
```
